# Optimizing a Trainium2 kernel written in Bass

```python
import numpy as np
import jax
import jax.numpy as jnp

def _softmax(x, axis=-1):
    return jax.nn.softmax(x, axis=axis)

def _gelu(x):
    return jax.nn.gelu(x, approximate=True)

def _silu(x):
    return jax.nn.silu(x)

def _sigmoid(x):
    return jax.nn.sigmoid(x)

def _layernorm(x, axis=-1, eps=1e-05):
    m = jnp.mean(x, axis=axis, keepdims=True)
    v = jnp.var(x, axis=axis, keepdims=True)
    return (x - m) / jnp.sqrt(v + eps)

def _scatter_add(tgt, idx, src, axis=0):
    return tgt.at[idx].add(src)

def _segment_sum(src, seg, n):
    return jax.ops.segment_sum(src, seg, n)
kernel_name = 'mk_lm_tower_d1_tok_ids512_r4_2c6bba'

def setup_inputs(seed: int=0):
    np.random.seed(seed)
    _w = jnp.asarray

    def _rec_inputs():
        import jax
        import jax.numpy as jnp
        _rk = jax.random.key(seed)
        x = jax.random.randint(jax.random.fold_in(_rk, 1), (8, 256), 0, 64, jnp.int32)
        return x
    x = _rec_inputs()

    def _L0_tok_setup():
        import jax, jax.numpy as jnp
        import numpy as np
        NGRAM_SIZES = (2, 3, 4)
        HASH_VOCAB = 25000
        EMBED_DIM = 128
        BATCH, SEQ = (8, 1024)

        def _ngram_hash_ids(byte_sequence, n):
            L = byte_sequence.shape[1] - n + 1
            h = jnp.zeros((byte_sequence.shape[0], L), dtype=jnp.int64)
            for j in range(n):
                h = (h * 64 + byte_sequence[:, j:j + L]) % HASH_VOCAB
            return h

        def _ngram_embed(byte_sequence, table, n):
            B, S = byte_sequence.shape
            ids = _ngram_hash_ids(byte_sequence, n)
            emb = table[ids]
            out = jnp.zeros((B, S, table.shape[1]), dtype=table.dtype)
            c = n // 2
            return out.at[:, c:c + emb.shape[1]].set(emb)
        key = jax.random.key(seed)
        ks = jax.random.split(key, 6)
        return {'byte_sequence': jax.random.randint(ks[0], (BATCH, SEQ), 0, 64, dtype=jnp.int64), 'emb_2': jax.random.normal(ks[1], (HASH_VOCAB, EMBED_DIM), dtype=jnp.float32), 'emb_3': jax.random.normal(ks[2], (HASH_VOCAB, EMBED_DIM), dtype=jnp.float32), 'emb_4': jax.random.normal(ks[3], (HASH_VOCAB, EMBED_DIM), dtype=jnp.float32), 'proj_w': jax.random.normal(ks[4], (EMBED_DIM, len(NGRAM_SIZES) * EMBED_DIM), dtype=jnp.float32) * 0.02, 'proj_b': jax.random.normal(ks[5], (EMBED_DIM,), dtype=jnp.float32) * 0.02}
    _L0_tok_all = _L0_tok_setup()
    _L0_tok_in = {k: v for k, v in _L0_tok_all.items() if k in ('emb_2', 'emb_3', 'emb_4', 'proj_w', 'proj_b')}
    del _L0_tok_all

    def _L0_attn_setup():
        import jax, jax.numpy as jnp
        import numpy as np
        CHUNK = 64
        THETA = 10000.0

        def rope2d(x):
            b, h, n, d = x.shape
            pad = -n % CHUNK
            if pad:
                x = jnp.pad(x, ((0, 0), (0, 0), (0, pad), (0, 0)))
            c = (n + pad) // CHUNK
            x = x.reshape(b, h, c, CHUNK, d)
            inv = 1.0 / THETA ** (jnp.arange(0, d, 4, dtype=jnp.float32) / d)
            fl = jnp.arange(CHUNK, dtype=jnp.float32)[:, None] * inv[None, :]
            cos_l, sin_l = (jnp.cos(fl), jnp.sin(fl))
            fc = jnp.arange(c, dtype=jnp.float32)[:, None] * inv[None, :]
            cos_c, sin_c = (jnp.cos(fc)[:, None, :], jnp.sin(fc)[:, None, :])
            x1, x2, x3, x4 = jnp.split(x, 4, axis=-1)
            r1 = x1 * cos_l - x2 * sin_l
            r2 = x1 * sin_l + x2 * cos_l
            r3 = x3 * cos_c - x4 * sin_c
            r4 = x3 * sin_c + x4 * cos_c
            out = jnp.concatenate([r1, r2, r3, r4], axis=-1).reshape(b, h, c * CHUNK, d)
            return out[:, :, :n]
        key = jax.random.key(seed)
        ks = jax.random.split(key, 6)
        dim, heads = (128, 8)
        b, n = (2, 512)
        s = 0.02
        return {'x': jax.random.normal(ks[0], (b, n, dim), dtype=jnp.float32), 'w_qkv': jax.random.normal(ks[1], (3 * dim, dim), dtype=jnp.float32) * s, 'b_qkv': jnp.zeros((3 * dim,), dtype=jnp.float32), 'w_pre': jax.random.normal(ks[2], (heads, heads), dtype=jnp.float32) * 0.3, 'w_post': jax.random.normal(ks[3], (heads, heads), dtype=jnp.float32) * 0.3, 'w_out': jax.random.normal(ks[4], (dim, dim), dtype=jnp.float32) * s, 'b_out': jnp.zeros((dim,), dtype=jnp.float32)}
    _L0_attn_all = _L0_attn_setup()
    _L0_attn_in = {k: v for k, v in _L0_attn_all.items() if k in ('w_qkv', 'b_qkv', 'w_pre', 'w_post', 'w_out', 'b_out')}
    del _L0_attn_all

    def _L0_ffn_setup():
        import jax, jax.numpy as jnp
        import numpy as np
        B, S, H = (4, 1024, 128)
        E, K = (64, 8)
        IE, IS = (128, 352)
        key = jax.random.key(seed)
        ks = jax.random.split(key, 8)
        scale = 0.02
        return {'x': jax.random.normal(ks[0], (B, S, H), jnp.float32), 'gate_w': jax.random.normal(ks[1], (E, H), jnp.float32) * scale, 'w1': jax.random.normal(ks[2], (E, H, IE), jnp.float32) * scale, 'w3': jax.random.normal(ks[3], (E, H, IE), jnp.float32) * scale, 'w2': jax.random.normal(ks[4], (E, IE, H), jnp.float32) * scale, 'sw1': jax.random.normal(ks[5], (H, IS), jnp.float32) * scale, 'sw3': jax.random.normal(ks[6], (H, IS), jnp.float32) * scale, 'sw2': jax.random.normal(ks[7], (IS, H), jnp.float32) * scale}
    _L0_ffn_all = _L0_ffn_setup()
    _L0_ffn_in = {k: v for k, v in _L0_ffn_all.items() if k in ('gate_w', 'w1', 'w3', 'w2', 'sw1', 'sw3', 'sw2')}
    del _L0_ffn_all
    return {'x': x, 'L0_tok_emb_2': _L0_tok_in['emb_2'], 'L0_tok_emb_3': _L0_tok_in['emb_3'], 'L0_tok_emb_4': _L0_tok_in['emb_4'], 'L0_tok_proj_w': _L0_tok_in['proj_w'], 'L0_tok_proj_b': _L0_tok_in['proj_b'], 'L0_attn_w_qkv': _L0_attn_in['w_qkv'], 'L0_attn_b_qkv': _L0_attn_in['b_qkv'], 'L0_attn_w_pre': _L0_attn_in['w_pre'], 'L0_attn_w_post': _L0_attn_in['w_post'], 'L0_attn_w_out': _L0_attn_in['w_out'], 'L0_attn_b_out': _L0_attn_in['b_out'], 'L0_ffn_gate_w': _L0_ffn_in['gate_w'], 'L0_ffn_w1': _L0_ffn_in['w1'], 'L0_ffn_w3': _L0_ffn_in['w3'], 'L0_ffn_w2': _L0_ffn_in['w2'], 'L0_ffn_sw1': _L0_ffn_in['sw1'], 'L0_ffn_sw3': _L0_ffn_in['sw3'], 'L0_ffn_sw2': _L0_ffn_in['sw2']}

def reference(x, L0_tok_emb_2, L0_tok_emb_3, L0_tok_emb_4, L0_tok_proj_w, L0_tok_proj_b, L0_attn_w_qkv, L0_attn_b_qkv, L0_attn_w_pre, L0_attn_w_post, L0_attn_w_out, L0_attn_b_out, L0_ffn_gate_w, L0_ffn_w1, L0_ffn_w3, L0_ffn_w2, L0_ffn_sw1, L0_ffn_sw3, L0_ffn_sw2):
    import jax
    import jax.numpy as jnp

    def _L0_tok_ref(byte_sequence, emb_2, emb_3, emb_4, proj_w, proj_b):
        import jax, jax.numpy as jnp
        import numpy as np
        NGRAM_SIZES = (2, 3, 4)
        HASH_VOCAB = 25000
        EMBED_DIM = 128
        BATCH, SEQ = (8, 1024)

        def _ngram_hash_ids(byte_sequence, n):
            L = byte_sequence.shape[1] - n + 1
            h = jnp.zeros((byte_sequence.shape[0], L), dtype=jnp.int64)
            for j in range(n):
                h = (h * 64 + byte_sequence[:, j:j + L]) % HASH_VOCAB
            return h

        def _ngram_embed(byte_sequence, table, n):
            B, S = byte_sequence.shape
            ids = _ngram_hash_ids(byte_sequence, n)
            emb = table[ids]
            out = jnp.zeros((B, S, table.shape[1]), dtype=table.dtype)
            c = n // 2
            return out.at[:, c:c + emb.shape[1]].set(emb)
        tables = (emb_2, emb_3, emb_4)
        combined = jnp.concatenate([_ngram_embed(byte_sequence, t, n) for t, n in zip(tables, NGRAM_SIZES)], axis=-1)
        return jnp.einsum('bsk,dk->bsd', combined, proj_w) + proj_b

    def _L0_attn_ref(x, w_qkv, b_qkv, w_pre, w_post, w_out, b_out):
        import jax, jax.numpy as jnp
        import numpy as np
        CHUNK = 64
        THETA = 10000.0

        def rope2d(x):
            b, h, n, d = x.shape
            pad = -n % CHUNK
            if pad:
                x = jnp.pad(x, ((0, 0), (0, 0), (0, pad), (0, 0)))
            c = (n + pad) // CHUNK
            x = x.reshape(b, h, c, CHUNK, d)
            inv = 1.0 / THETA ** (jnp.arange(0, d, 4, dtype=jnp.float32) / d)
            fl = jnp.arange(CHUNK, dtype=jnp.float32)[:, None] * inv[None, :]
            cos_l, sin_l = (jnp.cos(fl), jnp.sin(fl))
            fc = jnp.arange(c, dtype=jnp.float32)[:, None] * inv[None, :]
            cos_c, sin_c = (jnp.cos(fc)[:, None, :], jnp.sin(fc)[:, None, :])
            x1, x2, x3, x4 = jnp.split(x, 4, axis=-1)
            r1 = x1 * cos_l - x2 * sin_l
            r2 = x1 * sin_l + x2 * cos_l
            r3 = x3 * cos_c - x4 * sin_c
            r4 = x3 * sin_c + x4 * cos_c
            out = jnp.concatenate([r1, r2, r3, r4], axis=-1).reshape(b, h, c * CHUNK, d)
            return out[:, :, :n]
        b, n, dim = x.shape
        heads = w_pre.shape[0]
        d = dim // heads
        scale = d ** (-0.5)
        qkv = x @ w_qkv.T + b_qkv
        q, k, v = jnp.split(qkv, 3, axis=-1)

        def to_heads(t):
            return t.reshape(b, n, heads, d).transpose(0, 2, 1, 3)
        q, k, v = (to_heads(q), to_heads(k), to_heads(v))
        q = rope2d(q)
        k = rope2d(k)
        logits = jnp.einsum('bhid,bhjd->bhij', q, k) * scale
        logits = jnp.einsum('bhij,gh->bgij', logits, w_pre)
        attn = jax.nn.softmax(logits, axis=-1)
        attn = jnp.einsum('bhij,gh->bgij', attn, w_post)
        out = jnp.einsum('bhij,bhjd->bhid', attn, v)
        out = out.transpose(0, 2, 1, 3).reshape(b, n, dim)
        return out @ w_out.T + b_out

    def _L0_ffn_ref(x, gate_w, w1, w3, w2, sw1, sw3, sw2):
        import jax, jax.numpy as jnp
        import numpy as np
        B, S, H = (4, 1024, 128)
        E, K = (64, 8)
        IE, IS = (128, 352)
        b, s, h = x.shape
        xf = x.reshape(-1, h)
        T = xf.shape[0]
        logits = xf @ gate_w.T
        topk_w, topk_idx = jax.lax.top_k(logits, K)
        topk_w = jax.nn.softmax(topk_w, axis=-1)
        expert_flat = topk_idx.reshape(-1)
        order = jnp.argsort(expert_flat)
        group_sizes = jnp.bincount(expert_flat, length=E).astype(jnp.int32)
        tok_ids = (jnp.arange(T * K) // K)[order]
        xg = xf[tok_ids]
        hid = jax.nn.silu(jax.lax.ragged_dot(xg, w1, group_sizes)) * jax.lax.ragged_dot(xg, w3, group_sizes)
        y = jax.lax.ragged_dot(hid, w2, group_sizes)
        y = y * topk_w.reshape(-1)[order][:, None]
        routed = jnp.zeros_like(xf).at[tok_ids].add(y)
        shared = jax.nn.silu(xf @ sw1) * (xf @ sw3) @ sw2
        return (routed + shared).reshape(b, s, h)
    h = _L0_tok_ref(x, L0_tok_emb_2, L0_tok_emb_3, L0_tok_emb_4, L0_tok_proj_w, L0_tok_proj_b)
    h = h + _L0_attn_ref(_layernorm(h, axis=-1), L0_attn_w_qkv, L0_attn_b_qkv, L0_attn_w_pre, L0_attn_w_post, L0_attn_w_out, L0_attn_b_out)
    h = h + _L0_ffn_ref(_layernorm(h, axis=-1), L0_ffn_gate_w, L0_ffn_w1, L0_ffn_w3, L0_ffn_w2, L0_ffn_sw1, L0_ffn_sw3, L0_ffn_sw2)
    return h

_drawn_inputs = setup_inputs


def setup_inputs(seed=0):
    import zlib

    import numpy as np

    out = dict(_drawn_inputs(seed))
    spreads = {'L0_attn_b_qkv': (0.0, 0.1), 'L0_attn_b_out': (0.0, 0.1)}
    factors = {'L0_attn_w_qkv': 5.456,
     'L0_attn_w_pre': 8.0,
     'L0_ffn_gate_w': 8.0,
     'L0_ffn_w1': 8.0,
     'L0_ffn_w3': 8.0,
     'L0_ffn_w2': 8.0,
     'L0_ffn_sw1': 8.0,
     'L0_ffn_sw3': 8.0,
     'L0_ffn_sw2': 8.0}
    for name, (base, spread) in spreads.items():
        noise = np.random.default_rng([zlib.crc32(name.encode()), seed]).standard_normal(out[name].shape)
        drawn = base * np.exp(spread * noise) if base else spread * noise
        out[name] = jnp.asarray(drawn.astype(out[name].dtype))
    for name, factor in factors.items():
        out[name] = (out[name] * factor).astype(out[name].dtype)
    return out
```

```python
import numpy as np
import concourse.bass as bass
from concourse import mybir
from contextlib import ExitStack

B, S, D = 8, 256, 128
T = B * S
NH, DH = 8, 16
P = 128
NT = T // P
TPS = S // P
VOCAB, NGRAMS = 25000, 3
E, K, IE, IS = 64, 8, 128, 352
CAP = T + P
DUMMY = E * CAP
ROW = D + E + 1
TILES = T * K // P + E
ACCS = 4
RING = 8
SHC = 512
SHM = [(0, 128), (128, 128), (256, 96)]
BIG = 3.0e38

f32, bf16, i32 = mybir.dt.float32, mybir.dt.bfloat16, mybir.dt.int32
ALU, ACT, AX = mybir.AluOpType, mybir.ActivationFunctionType, mybir.AxisListType


def wait(eng, sem, value):
    if not isinstance(value, int) or value > 0:
        eng.wait_ge(sem, value)


class Count:

    def __init__(self, eng, sem, per, n):
        self.eng, self.sem, self.per, self.base, self.k = eng, sem, per, per * n, 0

    def __call__(self, ins):
        ins.then_inc(self.sem, 1)
        self.k += 1

    def wait(self):
        wait(self.eng, self.sem, self.base + self.k)

    def end(self):
        assert self.k == self.per, (self.k, self.per)


def tower(nc, x, emb2, emb3, emb4, w1, w3, w2, sw1, sw3, sw2, proj_t, qkv_t, out_t, gate_t,
          bias_rows, bias_cols, pre_cols, post_row, rope, consts, iotas, ids, out):
    with ExitStack() as ctx:
        def sb(name, shape, dt=f32):
            return ctx.enter_context(nc.sbuf_tensor(name, shape, dt))

        def sem(name):
            return ctx.enter_context(nc.semaphore(name))

        lists = nc.dram_tensor("lists", [DUMMY + P, ROW], f32).ap()
        acc = [nc.dram_tensor(f"acc{r}", [CAP, D], f32).ap() for r in range(ACCS)]

        w13_sb = sb("w13_sb", [P, E, 2 * IE])
        w2_sb = sb("w2_sb", [P, E, D])
        sw1_sb = sb("sw1_sb", [P, IS])
        sw3_sb = sb("sw3_sb", [P, IS])
        sw2_sb = sb("sw2_sb", [P, 3, D])
        proj_sb = sb("proj_sb", [P, NGRAMS, D])
        qkv_sb = sb("qkv_sb", [P, 5, D])
        outw_sb = sb("outw_sb", [P, D])
        gate_sb = sb("gate_sb", [P, E])
        brow = sb("brow", [1, 3, D])
        bcol = sb("bcol", [P, 4])
        pre_sb = sb("pre_sb", [P, NH])
        npre = sb("npre", [P, NH])
        post_sb = sb("post_sb", [P, NH, D])
        rope_sb = sb("rope_sb", [P, 2, S])
        const_sb = sb("const_sb", [P, 3 * P + E + ROW])
        ident, ones = const_sb[:, 0:P], const_sb[:, P:2 * P]
        before = const_sb[:, 2 * P:3 * P]
        base1 = const_sb[:, 3 * P:3 * P + E]
        pad = const_sb[:, 3 * P + E:3 * P + E + ROW]
        iota_sb = sb("iota_sb", [E, TILES + 16 + E])
        tile_no, tile_lo = iota_sb[:, 0:TILES], iota_sb[:, TILES:TILES + 16]
        upto = iota_sb[:, TILES + 16:TILES + 16 + E]
        ids_sb = sb("ids_sb", [P, NT], i32)
        ones_h = sb("ones_h", [P, P], bf16)
        before_h = sb("before_h", [P, P], bf16)

        xi = sb("xi", [B, S], i32)
        xf = sb("xf", [B, S + 4])
        hash_f = sb("hash_f", [B, NGRAMS, S + 1])
        quo = sb("quo", [B, S + 1], i32)
        quo_f = sb("quo_f", [B, S + 1])
        fix = sb("fix", [B, S + 1])
        idx_all = sb("idx_all", [P, B + 1, TPS * NGRAMS], i32)
        idx_cur = sb("idx_cur", [P, TPS * NGRAMS], i32)

        emb_g = sb("emb_g", [P, TPS * NGRAMS, D])
        emb_t = sb("emb_t", [P, NGRAMS, S])
        h_all = sb("h_all", [P, NT, D])
        stat = sb("stat", [P, 2, TPS, 6])
        mv = sb("mv", [P, 2, TPS, 2])
        nt = sb("nt", [P, 2, 3, TPS])
        xn = sb("xn", [P, TPS, D])
        xn_t = sb("xn_t", [P, S])
        rt = sb("rt", [P, 2, S])
        q_sb = sb("q_sb", [P, 2, S])
        k_sb = sb("k_sb", [P, 2, S])
        v_sb = sb("v_sb", [P, 2, TPS, D])

        qh = sb("qh", [P, 2, S])
        vh = sb("vh", [P, 4, TPS, D])
        neg_max = sb("neg_max", [P, 4, TPS])
        total = sb("total", [P, 4, TPS])
        inv = sb("inv", [P, 4, TPS])
        pr = sb("pr", [P, 4, TPS, S])
        pr_t = sb("pr_t", [P, 2, 2 * S])

        o_t = sb("o_t", [P, S])
        row = sb("row", [P, 2, TPS, ROW])
        xn2_cur = sb("xn2_cur", [P, S])
        xn2_t = sb("xn2_t", [P, T])
        top = sb("top", [P, TPS, 8])
        left = sb("left", [P, TPS, E])
        mask = sb("mask", [P, TPS, E], bf16)
        ntop = sb("ntop", [P, TPS])
        ex = sb("ex", [P, TPS, E])
        wsum = sb("wsum", [P, 2, TPS])
        cum = sb("cum", [P, E], bf16)
        posm = sb("posm", [P, TPS, E])
        pos8 = sb("pos8", [P, TPS, 8])
        pos = sb("pos", [P, 2, TPS, 8], i32)

        cnt = sb("cnt", [E, 1])
        ntiles = sb("ntiles", [E, 1])
        ends = sb("ends", [E, 1])
        gap = sb("gap", [E, 1])
        cmp16 = sb("cmp16", [E, 16])
        past = sb("past", [E, TILES])
        tab_e = sb("tab_e", [1, TILES + RING], i32)
        tab_off = sb("tab_off", [1, TILES], i32)
        offf = sb("offf", [1, TILES])
        tab_pad = sb("tab_pad", [1, E], i32)

        rows = sb("rows", [P, RING, ROW])
        x_t = sb("x_t", [P, 2, P])
        sg = sb("sg", [P, 2, IE])
        hid = sb("hid", [P, 2, IE])
        hid_t = sb("hid_t", [P, 2, P])
        y_sb = sb("y_sb", [P, RING, D])
        sh_g = pr[:, 0, :, :].rearrange("p a s -> p (a s)")
        sh_hid = pr[:, 1:4, :, :].rearrange("p m a s -> p m (a s)")
        acc_in = w13_sb[:, :, :].rearrange("p e n -> p (e n)")[:, 0:ACCS * NT * D] \
            .rearrange("p (r t d) -> p r t d", r=ACCS, t=NT)

        ps = ctx.enter_context(nc.psum_tensor("ps", [P, 8, 512], f32))
        SC, PT, OB, M0, M1, M2 = (0, 1), (2, 3), 4, 5, 6, 7

        L = sem("loaded_x"); LC = sem("loaded_consts"); LW = sem("loaded_experts"); LS = sem("loaded_shared")
        zeroed = sem("accumulators_zeroed")
        setup = sem("setup_done"); hashed = sem("hash_step"); hash_t = sem("hash_transposed"); idx_ok = sem("indices_ready")
        idx_n = sem("indices_of_sequence"); gathered = sem("rows_gathered")
        e_tr = sem("emb_transposed"); e_ev = sem("emb_evacuated"); e_zero = sem("emb_edges_zeroed")
        e_proj = sem("projected"); ln1 = sem("norm1_step"); e_xt = sem("norm1_transposed"); e_xe = sem("norm1_evacuated")
        v_mm = sem("v_product"); q_mm = sem("q_product"); k_mm = sem("k_product")
        v_ev = sem("v_ready"); q_rp = sem("q_rope_step"); k_rp = sem("k_rope_step")
        prep = sem("head_operands"); sc_mm = sem("scores"); mx = sem("score_max"); exd = sem("exponentials")
        nrm = sem("norm_step"); p_tr = sem("probs_transposed"); p_ev = sem("probs_evacuated"); pv = sem("values_summed")
        o_ev = sem("attended_evacuated"); o_mm = sem("attended_projected"); ln2 = sem("norm2_step")
        r_xt = sem("norm2_transposed"); r_xe = sem("norm2_evacuated"); g_mm = sem("gate_scores")
        tk = sem("topk_step"); g_ex = sem("gate_exponentials"); rk_mm = sem("ranks"); ps_s = sem("position_step")
        sent = [sem("rows_sent_even"), sem("rows_sent_odd")]; row_free = sem("row_buffer_free")
        c_mm = sem("counts"); tb = sem("table_step"); padded = sem("padding_written")
        shg = sem("shared_products"); sha = sem("shared_silu"); shh = sem("shared_hidden"); shy = sem("shared_out"); she = sem("shared_added")
        x_ld = [sem(f"tile_loaded{r}") for r in range(RING)]
        x_tr = sem("tile_transposed"); x_ev = sem("tile_evacuated"); h_mm = sem("hidden_product"); h_si = sem("silu_done")
        h_mu = sem("hidden_ready"); h_tr = sem("hidden_transposed"); h_ev = sem("hidden_evacuated"); y_mm = sem("expert_out")
        y_ev = sem("weighted_out"); added = [sem(f"scattered{r}") for r in range(ACCS)]
        acc_ld = sem("accumulators_loaded"); fin = sem("final_step"); stored = sem("stored"); passed = sem("wait_passed")
        block = ctx.enter_context(nc.Block())

        N_SETUP, N_HASH, N_LN1, N_LN2, N_TK, N_PS = 5, 20, 19, 20, 11, 7

        def hold(eng, sem_, value):
            if not isinstance(value, int) or value > 0:
                eng.wait_ge(sem_, value)
                eng.sem_inc(passed, 1)

        def front(eng, slot):
            for s in range(NH):
                slot(0, 0, s, True, False)
            with eng.Fori(0, 3) as j:
                for par in (1, 0):
                    for s in range(NH):
                        slot(2 * j + (1 if par else 2), par, s, True, True)
            for s in range(NH):
                slot(B - 1, 1, s, False, True)

        @block.sync
        def _(sp):
            sp.dma_start(xi[:, :], x).then_inc(L, 16)
            for dst, src in ((const_sb[:, :], consts), (iota_sb[:, :], iotas), (ids_sb[:, :], ids),
                             (proj_sb[:, :, :], proj_t.rearrange("(g p) d -> p g d", p=P)),
                             (qkv_sb[:, :, :], qkv_t.rearrange("p (a d) -> p a d", a=5)),
                             (brow[:, :, :], bias_rows.rearrange("(o a) d -> o a d", o=1)), (bcol[:, :], bias_cols),
                             (pre_sb[:, :], pre_cols), (rope_sb[:, :, :], rope.rearrange("a p s -> p a s")),
                             (post_sb[:, :, :], post_row.to_broadcast([P, NH, D])),
                             (outw_sb[:, :], out_t), (gate_sb[:, :], gate_t)):
                sp.dma_start(dst, src).then_inc(LC, 16)
            for dst, src in ((sw1_sb[:, :], sw1), (sw3_sb[:, :], sw3),
                             (sw2_sb[:, 0:2, :], sw2[0:2 * P, :].rearrange("(m p) d -> p m d", p=P)),
                             (sw2_sb[0:IS - 2 * P, 2, :], sw2[2 * P:IS, :])):
                sp.dma_start(dst, src).then_inc(LS, 16)
            sp.wait_ge(LC, 16 * 12)
            for r in range(ACCS):
                sp.dma_start(acc[r].rearrange("(a p) d -> p a d", p=P),
                             pad[:, 0:D].rearrange("p (o d) -> p o d", o=1).to_broadcast([P, CAP // P, D])).then_inc(zeroed, 16)
            for c in range(8):
                e = slice(8 * c, 8 * c + 8)
                sp.dma_start(w13_sb[:, e, 0:IE], w1[e].rearrange("e h i -> h e i")).then_inc(LW, 16)
                sp.dma_start(w13_sb[:, e, IE:2 * IE], w3[e].rearrange("e h i -> h e i")).then_inc(LW, 16)
                sp.dma_start(w2_sb[:, e, :], w2[e].rearrange("e i h -> i e h")).then_inc(LW, 16)
            sp.dma_start(lists[DUMMY:DUMMY + P, :], pad).then_inc(padded, 16)
            sp.wait_ge(tb, 8)
            with nc.sync.Fori(0, E) as e:
                at = nc.sync.value_load(tab_pad[0:1, bass.ds(e, 1)], min_val=0, max_val=DUMMY - P)
                sp.dma_start(lists[bass.ds(at, P), :], pad).then_inc(padded, 16)
            sp.wait_ge(padded, 16 * (E + 1))
            for par in range(2):
                sp.wait_ge(sent[par], 16 * TPS * K * (B // 2))
            sp.wait_ge(tb, 12)
            def load(i, r):
                at = nc.sync.value_load(tab_off[0:1, bass.ds(i, 1)], min_val=0, max_val=DUMMY)
                sp.dma_start(rows[:, r, :], lists[bass.ds(at, P), :]).then_inc(x_ld[r], 16)
            for r in range(RING):
                load(r, r)
            with nc.sync.Fori(1, TILES // RING) as j:
                for r in range(RING):
                    sp.wait_ge(added[r % ACCS], 16 * (2 * j - 1 + r // ACCS))
                    load(RING * j + r, r)
            for r in range(ACCS):
                sp.wait_ge(added[r], 16 * (TILES // ACCS))
                sp.dma_start(acc_in[:, r, :, :], acc[r][0:T, :].rearrange("(t p) d -> p t d", p=P)).then_inc(acc_ld, 16)
            for g in range(4):
                t = slice(4 * g, 4 * g + 4)
                sp.wait_ge(fin, ACCS * (g + 1))
                sp.dma_start(out.rearrange("b (c p) d -> p (b c) d", p=P)[:, t, :], h_all[:, t, :]).then_inc(stored, 16)
            sp.wait_ge(stored, 16 * 4)

        @block.gpsimd
        def _(pool):
            tables = (emb2, emb3, emb4)

            def gather(n):
                hold(pool, idx_n, n + 1)
                if not isinstance(n, int) or n > 0:
                    hold(pool, e_tr, TPS * n)
                for a in range(TPS * NGRAMS):
                    nc.gpsimd.indirect_dma_start(
                        out=emb_g[:, a, :], out_offset=None, in_=tables[a % NGRAMS],
                        in_offset=bass.IndirectOffsetOnAxis(ap=idx_cur[:, a:a + 1], axis=0)).then_inc(gathered, 16)

            def send(n, par):
                hold(pool, ps_s, N_PS * (n + 1))
                for it in range(TPS):
                    for c in range(K):
                        nc.gpsimd.indirect_dma_start(
                            out=lists, out_offset=bass.IndirectOffsetOnAxis(ap=pos[:, par, it, c:c + 1], axis=0),
                            in_=row[:, par, it, :], in_offset=None).then_inc(sent[par], 16)

            def free_rows(m):
                pool.wait_ge(sent[(m - 1) % 2] if isinstance(m, int) else m[0], 16 * TPS * K * ((m - 1) // 2 + 1 if isinstance(m, int) else m[1]))
                pool.sem_inc(row_free, 1)

            pool.sem_inc(row_free, 2)
            gather(0)
            gather(1)
            gather(2)
            gather(3)
            send(0, 0)
            with nc.gpsimd.Fori(0, 2) as j:
                gather(2 * j + 4)
                free_rows((sent[0], j + 1))
                send(2 * j + 1, 1)
                gather(2 * j + 5)
                free_rows((sent[1], j + 1))
                send(2 * j + 2, 0)
            for m in (5, 6, 7):
                free_rows(m)
                send(m, m % 2)
            pool.wait_ge(zeroed, 16 * ACCS)

            for r in range(RING):
                hold(pool, y_ev, r + 1)
                if r >= ACCS:
                    pool.wait_ge(added[r % ACCS], 16)
                nc.gpsimd.indirect_dma_start(
                    out=acc[r % ACCS], out_offset=bass.IndirectOffsetOnAxis(ap=rows[:, r, ROW - 1:ROW].bitcast(i32), axis=0),
                    in_=y_sb[:, r, :], in_offset=None, compute_op=ALU.add).then_inc(added[r % ACCS], 16)
            with nc.gpsimd.Fori(1, TILES // RING) as j:
                for r in range(RING):
                    hold(pool, y_ev, RING * j + r + 1)
                    hold(pool, added[r % ACCS], 16 * (2 * j + r // ACCS))
                    nc.gpsimd.indirect_dma_start(
                        out=acc[r % ACCS], out_offset=bass.IndirectOffsetOnAxis(ap=rows[:, r, ROW - 1:ROW].bitcast(i32), axis=0),
                        in_=y_sb[:, r, :], in_offset=None, compute_op=ALU.add).then_inc(added[r % ACCS], 16)

        @block.tensor
        def _(pe):
            mm = nc.tensor.matmul

            def embed_transpose(n):
                wait(pe, gathered, 16 * TPS * NGRAMS * (n + 1))
                wait(pe, k_rp, 3 * n)
                wait(pe, q_rp, 3 * n)
                for it in range(TPS):
                    for g in range(NGRAMS):
                        last = nc.tensor.transpose(ps[:, (M0, M1)[it], g * P:(g + 1) * P], emb_g[:, it * NGRAMS + g, :], ident)
                    last.then_inc(e_tr, 1)

            def project(n):
                wait(pe, e_zero, 3 * (n + 1))
                for it in range(TPS):
                    o = ps[:, M0, it * P:(it + 1) * P]
                    for g in range(NGRAMS):
                        mm(o, lhsT=emb_t[:, g, it * P:(it + 1) * P], rhs=proj_sb[:, g, :], start=(g == 0), stop=False)
                    last = mm(o, lhsT=ones[0:1, :], rhs=brow[0:1, 0, :], start=False, stop=True)
                last.then_inc(e_proj, 1)

            def norm1_transpose(n):
                wait(pe, ln1, N_LN1 * (n + 1))
                for it in range(TPS):
                    last = nc.tensor.transpose(ps[:, M1, it * P:(it + 1) * P], xn[:, it, :], ident)
                last.then_inc(e_xt, 1)

            def make_vq(n):
                wait(pe, e_xe, n + 1)
                for it in range(TPS):
                    o = ps[:, M0, it * P:(it + 1) * P]
                    mm(o, lhsT=xn_t[:, it * P:(it + 1) * P], rhs=qkv_sb[:, 4, :], start=True, stop=False)
                    last = mm(o, lhsT=ones[0:1, :], rhs=brow[0:1, 1, :], start=False, stop=True)
                last.then_inc(v_mm, 1)
                for a in range(2):
                    last = mm(ps[:, M1, a * S:(a + 1) * S], lhsT=qkv_sb[:, a, :], rhs=xn_t[:, :], start=True, stop=True)
                last.then_inc(q_mm, 1)

            def make_k(n):
                wait(pe, v_ev, n + 1)
                for a in range(2):
                    last = mm(ps[:, M0, a * S:(a + 1) * S], lhsT=qkv_sb[:, 2 + a, :], rhs=xn_t[:, :], start=True, stop=True)
                last.then_inc(k_mm, 1)

            def scores(b, par, h):
                wait(pe, prep, 2 * (NH * b + h + 1))
                wait(pe, exd, 2 * (NH * b + h - 1))
                for it in range(TPS):
                    last = mm(ps[:, SC[h % 2], it * S:(it + 1) * S], lhsT=qh[:, h % 2, it * P:(it + 1) * P],
                              rhs=k_sb[:, par, :], start=True, stop=True)
                last.then_inc(sc_mm, 1)

            def probs_transpose(u, h):
                wait(pe, nrm, 3 * (u + 1))
                wait(pe, p_ev, u - 1)
                for jt in range(2):
                    for it in range(TPS):
                        last = nc.tensor.transpose(ps[:, PT[h % 2], jt * S + it * P:jt * S + (it + 1) * P],
                                                   pr[:, h % 4, it, jt * P:(jt + 1) * P], ident)
                last.then_inc(p_tr, 1)

            def values(u, b, h):
                wait(pe, p_ev, u + 1)
                if h == 0:
                    wait(pe, o_ev, b)
                for jt in range(2):
                    last = mm(ps[:, OB, 0:S], lhsT=vh[:, h % 4, jt, :], rhs=pr_t[:, h % 2, jt * S:(jt + 1) * S],
                              start=(h == 0 and jt == 0), stop=(h == NH - 1 and jt == 1))
                last.then_inc(pv, 1)

            def out_project(n):
                wait(pe, o_ev, n + 1)
                for it in range(TPS):
                    o = ps[:, M2, it * P:(it + 1) * P]
                    mm(o, lhsT=o_t[:, it * P:(it + 1) * P], rhs=outw_sb[:, :], start=True, stop=False)
                    last = mm(o, lhsT=ones[0:1, :], rhs=brow[0:1, 2, :], start=False, stop=True)
                last.then_inc(o_mm, 1)

            def norm2_transpose(n, par):
                wait(pe, ln2, N_LN2 * (n + 1))
                for it in range(TPS):
                    last = nc.tensor.transpose(ps[:, M2, it * P:(it + 1) * P], row[:, par, it, 0:D], ident)
                last.then_inc(r_xt, 1)

            def gate(n):
                wait(pe, r_xe, n + 1)
                for it in range(TPS):
                    last = mm(ps[:, M2, it * E:(it + 1) * E], lhsT=xn2_cur[:, it * P:(it + 1) * P], rhs=gate_sb[:, :],
                              start=True, stop=True)
                last.then_inc(g_mm, 1)

            def rank(n):
                wait(pe, tk, N_TK * (n + 1))
                for it in range(TPS):
                    o = ps[:, M2, 128 + it * E:128 + (it + 1) * E]
                    mm(o, lhsT=before_h[:, :], rhs=mask[:, it, :], start=True, stop=False)
                    if it:
                        mm(o, lhsT=ones_h[:, :], rhs=mask[:, 0, :], start=False, stop=False)
                    last = mm(o, lhsT=ones_h[:, :], rhs=cum[:, :], start=False, stop=True)
                last.then_inc(rk_mm, 1)

            pe.wait_ge(LC, 16 * 12)
            pe.wait_ge(hashed, N_HASH)
            for it in range(TPS):
                for g in range(NGRAMS):
                    o = ps[:, M2, 0:B * TPS * NGRAMS].rearrange("p (b a) -> p b a", b=B)[:, :, it * NGRAMS + g]
                    s0 = it * P + (1 if g < 2 else 0)
                    last = mm(o, lhsT=hash_f[:, g, s0:s0 + P], rhs=ident[0:B, 0:B], start=True, stop=True)
            last.then_inc(hash_t, 1)
            pe.wait_ge(setup, N_SETUP)
            embed_transpose(0)
            project(0)
            norm1_transpose(0)
            make_vq(0)
            make_k(0)

            def slot(b, par, s, embeds, routes):
                scores(b, par, s)
                u = NH * b + s
                if routes or s >= 2:
                    probs_transpose(u - 2, (s - 2) % NH)
                if routes or s >= 3:
                    values(u - 3, b if s >= 3 else b - 1, (s - 3) % NH)
                if embeds and s == 0:
                    embed_transpose(b + 1)
                if embeds and s == 1:
                    project(b + 1)
                if embeds and s == 3:
                    norm1_transpose(b + 1)
                if routes and s == 3:
                    out_project(b - 1)
                if embeds and s == 4:
                    make_vq(b + 1)
                if embeds and s == 5:
                    make_k(b + 1)
                if routes and s == 5:
                    norm2_transpose(b - 1, 1 - par)
                if routes and s == 6:
                    gate(b - 1)
                if routes and s == 7:
                    rank(b - 1)

            front(nc.tensor, slot)
            U = NH * B
            probs_transpose(U - 2, 6)
            values(U - 3, B - 1, 5)
            probs_transpose(U - 1, 7)
            values(U - 2, B - 1, 6)
            values(U - 1, B - 1, 7)
            out_project(B - 1)
            norm2_transpose(B - 1, 1)
            gate(B - 1)
            rank(B - 1)

            pe.wait_ge(ps_s, N_PS * B)
            mm(ps[0:E, M0, 0:1], lhsT=cum[:, :], rhs=ones_h[:, 0:1], start=True, stop=True)
            mm(ps[0:1, M1, 0:E], lhsT=ones_h[:, 0:1], rhs=cum[:, :], start=True, stop=True).then_inc(c_mm, 1)
            pe.wait_ge(tb, 4)
            mm(ps[0:E, M2, 0:1], lhsT=upto, rhs=ntiles[:, :], start=True, stop=True).then_inc(c_mm, 1)
            pe.wait_ge(tb, 9)
            mm(ps[0:1, M0, 0:TILES], lhsT=ones[0:E, 0:1], rhs=past[:, :], start=True, stop=True)
            mm(ps[0:1, M1, 0:TILES], lhsT=gap[:, :], rhs=past[:, :], start=True, stop=True).then_inc(c_mm, 1)

            pe.wait_ge(LS, 16 * 4)
            pe.wait_ge(r_xe, B)
            def shared(c):
                for m, (lo, w) in enumerate(SHM):
                    k = 3 * c + m
                    wait(pe, shh, k - 1)
                    for a, wt in enumerate((sw1_sb, sw3_sb)):
                        last = mm(ps[0:w, 2 * (m % 2) + a, :], lhsT=wt[:, lo:lo + w], rhs=xn2_t[:, bass.ds(c * SHC, SHC)],
                                  start=True, stop=True)
                    last.then_inc(shg, 1)
                    if m == 1:
                        wait(pe, shh, k)
                wait(pe, shh, 3 * c + 3)
                wait(pe, she, c)
                for t in range(SHC // P):
                    for m, (lo, w) in enumerate(SHM):
                        last = mm(ps[:, OB, t * P:(t + 1) * P], lhsT=sh_hid[0:w, m, t * P:(t + 1) * P], rhs=sw2_sb[0:w, m, :],
                                  start=(m == 0), stop=(m == 2))
                last.then_inc(shy, 1)

            for c in range(T // SHC):
                shared(c)
            pe.wait_ge(she, T // SHC)

            pe.wait_ge(LW, 16 * 24)
            pe.wait_ge(tb, 12)

            def tile_transpose(i, r, j):
                wait(pe, x_ld[r], 16 * (j + 1))
                wait(pe, x_ev, i - 1)
                nc.tensor.transpose(ps[:, r % 2, 0:P], rows[:, r, 0:D], ident).then_inc(x_tr, 1)

            def hidden(i, r, e):
                wait(pe, x_ev, i + 1)
                wait(pe, h_mu, i - 1)
                mm(ps[:, 2 + r % 2, 0:2 * IE], lhsT=x_t[:, r % 2, :],
                   rhs=w13_sb[:, bass.ds(e, 1), :].rearrange("p a n -> p (a n)"), start=True, stop=True).then_inc(h_mm, 1)

            def hidden_transpose(i, r):
                wait(pe, h_mu, i + 1)
                wait(pe, h_ev, i - 1)
                nc.tensor.transpose(ps[:, 4 + r % 2, 0:P], hid[:, r % 2, :], ident).then_inc(h_tr, 1)

            def down(i, r, e):
                wait(pe, h_ev, i + 1)
                wait(pe, y_ev, i - 1)
                mm(ps[:, 6 + r % 2, 0:D], lhsT=hid_t[:, r % 2, :],
                   rhs=w2_sb[:, bass.ds(e, 1), :].rearrange("p a n -> p (a n)"), start=True, stop=True).then_inc(y_mm, 1)

            def eight(j, first, last):
                i = RING * j
                e = [nc.tensor.value_load(tab_e[0:1, bass.ds(i + d, 1)], min_val=0, max_val=E - 1) for d in range(RING + 2)]
                if first:
                    tile_transpose(0, 0, 0)
                    tile_transpose(1, 1, 0)
                    hidden(0, 0, e[1])
                for r in range(RING):
                    if not (last and r >= RING - 2):
                        tile_transpose(i + r + 2, (r + 2) % RING, j + (r + 2) // RING)
                    if not (last and r == RING - 1):
                        hidden(i + r + 1, (r + 1) % RING, e[r + 2])
                    hidden_transpose(i + r, r)
                    if not (first and r == 0):
                        down(i + r - 1, (r - 1) % RING, e[r])
                if last:
                    down(i + RING - 1, RING - 1, e[RING])

            eight(0, True, False)
            with nc.tensor.Fori(1, TILES // RING - 1) as j:
                eight(j, False, False)
            eight(TILES // RING - 1, False, True)

        @block.scalar
        def _(act):
            copy = ACT.Copy

            def embed_evac(n):
                for it in range(TPS):
                    wait(act, e_tr, TPS * n + it + 1)
                    if it == 0:
                        wait(act, e_proj, n)
                    nc.scalar.activation(emb_t[:, :, it * P:(it + 1) * P],
                                         ps[:, (M0, M1)[it], 0:NGRAMS * P].rearrange("p (g t) -> p g t", g=NGRAMS), copy).then_inc(e_ev, 1)

            def norm1_evac(n):
                wait(act, e_xt, n + 1)
                wait(act, k_mm, n)
                nc.scalar.activation(xn_t[:, :], ps[:, M1, 0:S], copy).then_inc(e_xe, 1)

            def exps(u, h):
                wait(act, mx, u + 1)
                wait(act, p_tr, u - 3)
                for it in range(TPS):
                    nc.scalar.activation(pr[:, h % 4, it, :], ps[:, SC[h % 2], it * S:(it + 1) * S], ACT.Exp,
                                         bias=neg_max[:, h % 4, it:it + 1], scale=-1.0,
                                         accum_out=total[:, h % 4, it:it + 1]).then_inc(exd, 1)

            def probs_evac(u, h):
                wait(act, p_tr, u + 1)
                wait(act, pv, u - 1)
                nc.scalar.activation(pr_t[:, h % 2, :], ps[:, PT[h % 2], :], copy).then_inc(p_ev, 1)

            def attended_evac(n):
                wait(act, pv, NH * (n + 1))
                nc.scalar.activation(o_t[:, :], ps[:, OB, 0:S], copy).then_inc(o_ev, 1)

            def norm2_evac(n):
                wait(act, r_xt, n + 1)
                nc.scalar.activation(xn2_t[:, bass.ds(n * S, S)], ps[:, M2, 0:S], copy)
                nc.scalar.activation(xn2_cur[:, :], ps[:, M2, 0:S], copy).then_inc(r_xe, 1)

            def gate_exps(n):
                wait(act, tk, N_TK * n + 6)
                for it in range(TPS):
                    nc.scalar.activation(ex[:, it, :], ps[:, M2, it * E:(it + 1) * E], ACT.Exp,
                                         bias=ntop[:, it:it + 1], scale=1.0).then_inc(g_ex, 1)

            embed_evac(0)
            norm1_evac(0)

            def slot(b, par, s, embeds, routes):
                u = NH * b + s
                exps(u, s)
                if routes or s >= 2:
                    probs_evac(u - 2, (s - 2) % NH)
                if embeds and s == 0:
                    embed_evac(b + 1)
                if embeds and s == 3:
                    norm1_evac(b + 1)
                if routes and s == 2:
                    attended_evac(b - 1)
                if routes and s == 5:
                    norm2_evac(b - 1)
                if routes and s == 6:
                    gate_exps(b - 1)

            front(nc.scalar, slot)
            U = NH * B
            probs_evac(U - 2, 6)
            probs_evac(U - 1, 7)
            attended_evac(B - 1)
            norm2_evac(B - 1)
            gate_exps(B - 1)

            for c in range(T // SHC):
                for m, (lo, w) in enumerate(SHM):
                    wait(act, shg, 3 * c + m + 1)
                    wait(act, shh, 3 * c + m)
                    nc.scalar.activation(sh_g[0:w, :], ps[0:w, 2 * (m % 2), :], ACT.Silu).then_inc(sha, 1)

            def silu(i, r):
                wait(act, h_mm, i + 1)
                wait(act, h_mu, i - 1)
                nc.scalar.activation(sg[:, r % 2, :], ps[:, 2 + r % 2, 0:IE], ACT.Silu).then_inc(h_si, 1)

            def hid_evac(i, r):
                wait(act, h_tr, i + 1)
                wait(act, y_mm, i - 1)
                nc.scalar.activation(hid_t[:, r % 2, :], ps[:, 4 + r % 2, 0:P], copy).then_inc(h_ev, 1)

            def eight(j, last):
                for r in range(RING):
                    if not (last and r == RING - 1):
                        silu(RING * j + r + 1, (r + 1) % RING)
                    hid_evac(RING * j + r, r)

            silu(0, 0)
            eight(0, False)
            with nc.scalar.Fori(1, TILES // RING - 1) as j:
                eight(j, False)
            eight(TILES // RING - 1, True)

        @block.vector
        def _(dve):
            v = nc.vector

            def rsqrt(st, n, which):
                var, y, a = nt[:, which, 0, :], nt[:, which, 1, :], nt[:, which, 2, :]
                st.wait()
                st(v.tensor_scalar(var, mv[:, which, :, 1], 1e-5, None, ALU.add))
                st.wait()
                st(v.tensor_scalar(a.bitcast(i32), var.bitcast(i32), 1, None, ALU.arith_shift_right))
                st.wait()
                st(v.tensor_scalar(y.bitcast(i32), a.bitcast(i32), -1.0, float(0x5F3759DF), ALU.mult, ALU.add))
                for _ in range(3):
                    st.wait()
                    st(v.tensor_tensor(a, y, y, ALU.mult))
                    st.wait()
                    st(v.scalar_tensor_tensor(out=a, in0=a, scalar=-0.5, in1=var, op0=ALU.mult, op1=ALU.mult))
                    st.wait()
                    st(v.scalar_tensor_tensor(out=y, in0=a, scalar=1.5, in1=y, op0=ALU.add, op1=ALU.mult))
                st.wait()

            def indices(n):
                if not isinstance(n, int) or n > 0:
                    wait(dve, gathered, 16 * TPS * NGRAMS * n)
                    v.tensor_scalar(idx_cur[:, :], idx_all[:, bass.ds(n, 1), :].rearrange("p o a -> p (o a)"), 0, None, ALU.add).then_inc(idx_n, 1)
                else:
                    v.tensor_copy(idx_cur[:, :], idx_all[:, 0, :]).then_inc(idx_n, 1)

            def edges(n):
                wait(dve, e_ev, TPS * (n + 1))
                v.memset(emb_t[:, 0:3, 0:1], 0.0).then_inc(e_zero, 1)
                v.memset(emb_t[:, 1:3, S - 1:S], 0.0).then_inc(e_zero, 1)
                v.memset(emb_t[:, 2:3, 1:2], 0.0).then_inc(e_zero, 1)

            def norm1(n):
                st = Count(dve, ln1, N_LN1, n)
                wait(dve, e_proj, n + 1)
                wait(dve, e_xt, n)
                src = ps[:, M0, 0:TPS * D].rearrange("p (t d) -> p t d", t=TPS)
                st(v.tensor_scalar(h_all[:, bass.ds(TPS * n, TPS), :], src, 0.0, None, ALU.add))
                for it in range(TPS):
                    st(v.bn_stats(stat[:, 0, it, :], src[:, it, :]))
                hold(dve, ln1, st.base + st.k)
                for it in range(TPS):
                    st(v.bn_aggr(mv[:, 0, it, :], stat[:, 0, it, :]))
                rsqrt(st, n, 0)
                for it in range(TPS):
                    st(v.tensor_scalar(xn[:, it, :], src[:, it, :], mv[:, 0, it, 0:1], nt[:, 0, 1, it:it + 1], ALU.subtract, ALU.mult))
                st.end()

            def evac_v(n, par):
                wait(dve, v_mm, n + 1)
                wait(dve, prep, 2 * NH * (n - 1))
                v.tensor_scalar(v_sb[:, par, :, :].rearrange("p t d -> p (t d)"), ps[:, M0, 0:TPS * D], 0.0, None, ALU.add).then_inc(v_ev, 1)

            def rotate(n, par, src_sem, sem_, bank, dst, col):
                st = Count(dve, sem_, 3, n)
                wait(dve, src_sem, n + 1)
                if dst is q_sb:
                    wait(dve, k_rp, 3 * n)
                else:
                    wait(dve, q_rp, 3 * (n + 1))
                    wait(dve, sc_mm, NH * (n - 1))
                for a in range(2):
                    st(v.scalar_tensor_tensor(out=rt[:, a, :], in0=ps[:, bank, a * S:(a + 1) * S], scalar=bcol[:, col + a:col + a + 1],
                                              in1=rope_sb[:, a, :], op0=ALU.add, op1=ALU.mult))
                st.wait()
                st(v.tensor_tensor(dst[:, par, :], rt[:, 0, :], rt[:, 1, :], ALU.add))
                st.end()

            def prepare(b, par, h):
                u = NH * b + h
                wait(dve, k_rp, 3 * (b + 1))
                wait(dve, q_rp, 3 * (b + 1))
                wait(dve, v_ev, b + 1)
                wait(dve, sc_mm, u - 1)
                wait(dve, pv, u - 3)
                v.tensor_scalar(qh[:, h % 2, :], q_sb[:, par, :], npre[:, h:h + 1], None, ALU.mult).then_inc(prep, 1)
                v.tensor_tensor(vh[:, h % 4, :, :], v_sb[:, par, :, :],
                                post_sb[:, h:h + 1, :].to_broadcast([P, TPS, D]), ALU.mult).then_inc(prep, 1)

            def maxima(u, h):
                wait(dve, sc_mm, u + 1)
                wait(dve, exd, 2 * (u - 3))
                v.tensor_reduce(neg_max[:, h % 4, :], ps[:, SC[h % 2], :].rearrange("p (t s) -> p t s", t=TPS), AX.X, ALU.min).then_inc(mx, 1)

            def normalise(u, h):
                wait(dve, exd, 2 * (u + 1))
                v.reciprocal(inv[:, h % 4, :], total[:, h % 4, :]).then_inc(nrm, 1)
                wait(dve, nrm, 3 * u + 1)
                for it in range(TPS):
                    v.tensor_scalar(pr[:, h % 4, it, :], pr[:, h % 4, it, :], inv[:, h % 4, it:it + 1], None, ALU.mult).then_inc(nrm, 1)

            def residual_norm2(n, par):
                st = Count(dve, ln2, N_LN2, n)
                hs = h_all[:, bass.ds(TPS * n, TPS), :]
                wait(dve, o_mm, n + 1)
                wait(dve, ln1, N_LN1 * (n + 1))
                wait(dve, row_free, n + 1)
                st(v.tensor_tensor(hs, ps[:, M2, 0:TPS * D].rearrange("p (t d) -> p t d", t=TPS), hs, ALU.add))
                hold(dve, ln2, st.base + st.k)
                for it in range(TPS):
                    st(v.bn_stats(stat[:, 1, it, :], h_all[:, bass.ds(TPS * n + it, 1), :].rearrange("p o d -> p (o d)")))
                hold(dve, ln2, st.base + st.k)
                for it in range(TPS):
                    st(v.bn_aggr(mv[:, 1, it, :], stat[:, 1, it, :]))
                rsqrt(st, n, 1)
                for it in range(TPS):
                    st(v.tensor_scalar(row[:, par, it, 0:D], h_all[:, bass.ds(TPS * n + it, 1), :].rearrange("p o d -> p (o d)"),
                                       mv[:, 1, it, 0:1], nt[:, 1, 1, it:it + 1], ALU.subtract, ALU.mult))
                st(v.tensor_copy(row[:, par, :, ROW - 1:ROW].bitcast(i32), ids_sb[:, bass.ds(TPS * n, TPS)].rearrange("p (t o) -> p t o", o=1)))
                st.end()

            def choose(n, par):
                st = Count(dve, tk, N_TK, n)
                lg = ps[:, M2, 0:TPS * E].rearrange("p (t e) -> p t e", t=TPS)
                hold(dve, g_mm, n + 1)
                for it in range(TPS):
                    st(v.max(top[:, it, :], lg[:, it, :]))
                hold(dve, tk, st.base + st.k)
                for it in range(TPS):
                    st(v.match_replace(left[:, it, :], top[:, it, :], lg[:, it, :], -BIG))
                st.wait()
                st(v.tensor_tensor(mask[:, :, :], left[:, :, :], lg, ALU.not_equal))
                st(v.tensor_scalar(ntop[:, :], top[:, :, 0], -1.0, None, ALU.mult))
                wait(dve, g_ex, TPS * (n + 1))
                st.wait()
                for it in range(TPS):
                    st(v.scalar_tensor_tensor(out=ex[:, it, :], in0=ex[:, it, :], scalar=1.0, in1=mask[:, it, :], op0=ALU.mult, op1=ALU.mult,
                                              accum_out=wsum[:, 0, it:it + 1]))
                st.wait()
                st(v.reciprocal(wsum[:, 1, :], wsum[:, 0, :]))
                st.wait()
                for it in range(TPS):
                    st(v.tensor_scalar(row[:, par, it, D:D + E], ex[:, it, :], wsum[:, 1, it:it + 1], None, ALU.mult))
                st.end()

            def place(n, par):
                st = Count(dve, ps_s, N_PS, n)
                rk = ps[:, M2, 128:128 + TPS * E].rearrange("p (t e) -> p t e", t=TPS)
                wait(dve, rk_mm, n + 1)
                st(v.tensor_tensor(posm[:, :, :], rk, base1.rearrange("p (o e) -> p o e", o=1).to_broadcast([P, TPS, E]), ALU.add))
                st(v.tensor_tensor(cum[:, :], cum[:, :], mask[:, 0, :], ALU.add))
                st.wait()
                st(v.tensor_tensor(posm[:, :, :], posm[:, :, :], mask[:, :, :], ALU.mult))
                st(v.tensor_tensor(cum[:, :], cum[:, :], mask[:, 1, :], ALU.add))
                hold(dve, ps_s, st.base + st.k)
                for it in range(TPS):
                    st(v.max(pos8[:, it, :], posm[:, it, :]))
                st.wait()
                st(v.tensor_scalar(pos[:, par, :, :], pos8[:, :, :], -1.0, None, ALU.add))
                st.end()

            hs = [0]

            def link(ins):
                hs[0] += 1
                ins.then_inc(hashed, 1)
                dve.wait_ge(hashed, hs[0])

            link(v.memset(xf[:, :], 0.0))
            dve.wait_ge(L, 16)
            link(v.tensor_copy(xf[:, 2:2 + S], xi[:, :]))
            W = S + 1
            link(v.scalar_tensor_tensor(out=hash_f[:, 0, :], in0=xf[:, 0:W], scalar=64.0, in1=xf[:, 1:1 + W], op0=ALU.mult, op1=ALU.add))
            link(v.scalar_tensor_tensor(out=hash_f[:, 1, :], in0=hash_f[:, 0, :], scalar=64.0, in1=xf[:, 2:2 + W], op0=ALU.mult, op1=ALU.add))

            def modulo(a):
                link(v.tensor_scalar(quo[:, :], a, 1.0 / VOCAB, None, ALU.mult))
                link(v.tensor_copy(quo_f[:, :], quo[:, :]))
                link(v.scalar_tensor_tensor(out=a, in0=quo_f[:, :], scalar=-float(VOCAB), in1=a, op0=ALU.mult, op1=ALU.add))
                link(v.tensor_scalar(fix[:, :], a, 0.0, float(VOCAB), ALU.is_lt, ALU.mult))
                link(v.tensor_tensor(a, a, fix[:, :], ALU.add))
                link(v.tensor_scalar(fix[:, :], a, float(VOCAB), -float(VOCAB), ALU.is_ge, ALU.mult))
                link(v.tensor_tensor(a, a, fix[:, :], ALU.add))

            modulo(hash_f[:, 1, :])
            link(v.memset(hash_f[:, 2, S:W], 0.0))
            link(v.scalar_tensor_tensor(out=hash_f[:, 2, 0:S], in0=hash_f[:, 1, 0:S], scalar=64.0, in1=xf[:, 3:3 + S], op0=ALU.mult, op1=ALU.add))
            modulo(hash_f[:, 2, :])
            dve.wait_ge(hash_t, 1)
            v.tensor_copy(idx_all[:, 0:B, :].rearrange("p b a -> p (b a)"), ps[:, M2, 0:B * TPS * NGRAMS]).then_inc(idx_ok, 1)
            v.memset(idx_all[:, B, :], 0).then_inc(idx_ok, 1)
            dve.wait_ge(idx_ok, 2)
            indices(0)
            dve.wait_ge(LC, 16 * 12)
            v.tensor_scalar(npre[:, :], pre_sb[:, :], -float(DH) ** -0.5, None, ALU.mult).then_inc(setup, 1)
            v.tensor_copy(ones_h[:, :], ones).then_inc(setup, 1)
            v.tensor_copy(before_h[:, :], before).then_inc(setup, 1)
            v.memset(cum[:, :], 0.0).then_inc(setup, 1)
            v.memset(tab_e[:, :], 0).then_inc(setup, 1)
            dve.wait_ge(setup, N_SETUP)
            edges(0)
            indices(1)
            norm1(0)
            evac_v(0, 0)
            rotate(0, 0, q_mm, q_rp, M1, q_sb, 0)
            rotate(0, 0, k_mm, k_rp, M0, k_sb, 2)
            prepare(0, 0, 0)

            def slot(b, par, s, embeds, routes):
                u = NH * b + s
                if s < NH - 1:
                    prepare(b, par, s + 1)
                maxima(u, s)
                if routes or s >= 1:
                    normalise(u - 1, (s - 1) % NH)
                if embeds and s == 0:
                    edges(b + 1)
                    indices(b + 2)
                if embeds and s == 1:
                    norm1(b + 1)
                if routes and s == 3:
                    residual_norm2(b - 1, 1 - par)
                if embeds and s == 4:
                    evac_v(b + 1, 1 - par)
                    rotate(b + 1, 1 - par, q_mm, q_rp, M1, q_sb, 0)
                if embeds and s == 5:
                    rotate(b + 1, 1 - par, k_mm, k_rp, M0, k_sb, 2)
                if routes and s == 6:
                    choose(b - 1, 1 - par)
                if routes and s == 7:
                    place(b - 1, 1 - par)
                if embeds and s == NH - 1:
                    prepare(b + 1, 1 - par, 0)

            front(nc.vector, slot)
            U = NH * B
            normalise(U - 1, 7)
            residual_norm2(B - 1, 1)
            choose(B - 1, 1)
            place(B - 1, 1)

            tk_ = [0]

            def table(ins):
                tk_[0] += 1
                ins.then_inc(tb, 1)
                dve.wait_ge(tb, tk_[0])

            dve.wait_ge(c_mm, 1)
            table(v.tensor_copy(cnt[:, :], ps[0:E, M0, 0:1]))
            table(v.tensor_tensor(offf[0:1, 0:E], ps[0:1, M1, 0:E], base1[0:1, :], ALU.add))
            table(v.tensor_scalar(cmp16[:, :], tile_lo, cnt[:, 0:1], None, ALU.is_lt))
            table(v.tensor_reduce(ntiles[:, :], cmp16[:, :], AX.X, ALU.add))
            table(v.tensor_scalar(gap[:, :], ntiles[:, :], -float(P), float(CAP), ALU.mult, ALU.add))
            table(v.tensor_scalar(tab_pad[:, :], offf[0:1, 0:E], -1.0, None, ALU.add))
            dve.wait_ge(c_mm, 2)
            table(v.tensor_copy(ends[:, :], ps[0:E, M2, 0:1]))
            table(v.memset(cmp16[:, 0:1], 0.0))
            table(v.tensor_scalar(past[:, :], tile_no, ends[:, 0:1], None, ALU.is_ge))
            dve.wait_ge(c_mm, 3)
            table(v.scalar_tensor_tensor(out=offf[:, :], in0=tile_no[0:1, :], scalar=float(P), in1=ps[0:1, M1, 0:TILES], op0=ALU.mult, op1=ALU.add))
            table(v.tensor_scalar(tab_off[:, :], offf[:, :], float(DUMMY), None, ALU.min))
            table(v.tensor_scalar(tab_e[:, 1:1 + TILES], ps[0:1, M0, 0:TILES], float(E - 1), None, ALU.min))

            for c in range(T // SHC):
                for m, (lo, w) in enumerate(SHM):
                    wait(dve, sha, 3 * c + m + 1)
                    wait(dve, shy, c)
                    v.tensor_tensor(sh_hid[0:w, m, :], sh_g[0:w, :], ps[0:w, 2 * (m % 2) + 1, :], ALU.mult).then_inc(shh, 1)
                wait(dve, shy, c + 1)
                hc = h_all[:, c * (SHC // P):(c + 1) * (SHC // P), :].rearrange("p t d -> p (t d)")
                v.tensor_tensor(hc, ps[:, OB, :], hc, ALU.add).then_inc(she, 1)

            def tile_evac(i, r):
                wait(dve, x_tr, i + 1)
                wait(dve, h_mm, i - 1)
                v.tensor_copy(x_t[:, r % 2, :], ps[:, r % 2, 0:P]).then_inc(x_ev, 1)

            def gated(i, r):
                wait(dve, h_si, i + 1)
                wait(dve, h_tr, i - 1)
                v.tensor_tensor(hid[:, r % 2, :], sg[:, r % 2, :], ps[:, 2 + r % 2, IE:2 * IE], ALU.mult).then_inc(h_mu, 1)

            def weighted(i, r, e):
                wait(dve, y_mm, i + 1)
                v.tensor_scalar(y_sb[:, r, :], ps[:, 6 + r % 2, 0:D], rows[:, r, bass.ds(e + D, 1)], None, ALU.mult).then_inc(y_ev, 1)

            def eight(j, first, last):
                i = RING * j
                e = [nc.vector.value_load(tab_e[0:1, bass.ds(i + d, 1)], min_val=0, max_val=E - 1) for d in range(RING + 1)]
                if first:
                    tile_evac(0, 0)
                    tile_evac(1, 1)
                    gated(0, 0)
                for r in range(RING):
                    if not (last and r >= RING - 2):
                        tile_evac(i + r + 2, (r + 2) % RING)
                    if not (last and r == RING - 1):
                        gated(i + r + 1, (r + 1) % RING)
                    if not (first and r == 0):
                        weighted(i + r - 1, (r - 1) % RING, e[r])
                if last:
                    weighted(i + RING - 1, RING - 1, e[RING])

            dve.wait_ge(x_ld[0], 16)
            eight(0, True, False)
            with nc.vector.Fori(1, TILES // RING - 1) as j:
                eight(j, False, False)
            eight(TILES // RING - 1, False, True)

            dve.wait_ge(acc_ld, 16 * ACCS)
            for g in range(4):
                t = slice(4 * g, 4 * g + 4)
                for r in range(ACCS):
                    if r:
                        dve.wait_ge(fin, ACCS * g + r)
                    v.tensor_tensor(h_all[:, t, :], h_all[:, t, :], acc_in[:, r, t, :], ALU.add).then_inc(fin, 1)


_OUT = (B, S, D)


def kernel(**inputs):
    import concourse.bacc as bacc
    from concourse.bass_utils import run_bass_kernel_spmd as run

    g = {k: np.asarray(a) for k, a in inputs.items()}
    f = np.float32
    wq, wk, wv = (g["L0_attn_w_qkv"][i * D:(i + 1) * D] for i in range(3))
    bq, bk, bv = (g["L0_attn_b_qkv"][i * D:(i + 1) * D] for i in range(3))
    swap = np.arange(D).reshape(NH, 4, DH // 4)[:, [1, 0, 3, 2]].reshape(D)
    inv = (1.0 / 10000.0 ** (np.arange(0, DH, 4, dtype=f) / DH)).astype(f)
    pos = np.arange(S, dtype=f)
    local = (pos % 64)[None, :] * inv[:, None]
    chunk = np.floor(pos / 64)[None, :] * inv[:, None]
    ang = np.stack([local, local, chunk, chunk])
    sign = np.array([-1, 1, -1, 1], f)[:, None, None]
    rope = np.stack([np.tile(np.cos(ang).reshape(DH, S), (NH, 1)),
                     np.tile((sign * np.sin(ang)).reshape(DH, S), (NH, 1))]).astype(f)
    p = np.arange(P)
    padding = np.zeros((P, ROW), f)
    padding[:, ROW - 1] = (T + p).astype(np.int32).view(f)
    consts = np.concatenate([np.eye(P, dtype=f), np.ones((P, P), f), (p[:, None] < p[None, :]).astype(f),
                             np.tile((np.arange(E) * CAP + 1).astype(f), (P, 1)), padding], axis=1)
    e = np.arange(E)
    iotas = np.concatenate([np.tile(np.arange(TILES, dtype=f), (E, 1)), np.tile(P * np.arange(16, dtype=f), (E, 1)),
                            (e[:, None] <= e[None, :]).astype(f)], axis=1)
    args = {
        "x": g["x"], "emb2": g["L0_tok_emb_2"], "emb3": g["L0_tok_emb_3"], "emb4": g["L0_tok_emb_4"],
        "w1": g["L0_ffn_w1"], "w3": g["L0_ffn_w3"], "w2": g["L0_ffn_w2"],
        "sw1": g["L0_ffn_sw1"], "sw3": g["L0_ffn_sw3"], "sw2": g["L0_ffn_sw2"],
        "proj_t": g["L0_tok_proj_w"].T,
        "qkv_t": np.concatenate([wq.T, wq[swap].T, wk.T, wk[swap].T, wv.T], axis=1),
        "out_t": g["L0_attn_w_out"].T, "gate_t": g["L0_ffn_gate_w"].T,
        "bias_rows": np.stack([g["L0_tok_proj_b"], bv, g["L0_attn_b_out"]]),
        "bias_cols": np.stack([bq, bq[swap], bk, bk[swap]], axis=1),
        "pre_cols": np.repeat(g["L0_attn_w_pre"].T, DH, axis=0),
        "post_row": np.repeat(g["L0_attn_w_post"].T, DH, axis=1).reshape(1, NH, D),
        "rope": rope, "consts": consts, "iotas": iotas,
        "ids": (np.arange(NT)[None, :] * P + p[:, None]).astype(np.int32),
    }
    nc = bacc.Bacc("TRN2", target_bir_lowering=False, num_devices=1)
    arrays, aps = {}, []
    for name, a in args.items():
        a = np.ascontiguousarray(a)
        arrays[f"in_{name}"] = a
        aps.append(nc.dram_tensor(f"in_{name}", a.shape, mybir.dt.from_np(a.dtype), kind="ExternalInput").ap())
    aps.append(nc.dram_tensor("out_0", _OUT, f32, kind="ExternalOutput").ap())
    tower(nc, *aps)
    r = run(nc, [arrays], core_ids=[0])
    return r.results[0]["out_0"]
```

```python
import numpy as np
import concourse.bass as bass
from concourse import mybir
from contextlib import ExitStack

B, S, D = 8, 256, 128
T = B * S
NH, DH = 8, 16
P = 128
NT = T // P
TPS = S // P
VOCAB, NGRAMS = 25000, 3
E, K, IE, IS = 64, 8, 128, 352
CAP = T + P
DUMMY = E * CAP
ROW = D + E + 1
TILES = T * K // P + E
ACCS = 4
RING = 16
PAIRS = RING // 2
GROUPS = TILES // RING
PER_ACC = RING // ACCS
SHC = 512
SHM = [(0, 128), (128, 128), (256, 96)]
BIG = 3.0e38

f32, bf16, i32 = mybir.dt.float32, mybir.dt.bfloat16, mybir.dt.int32
ALU, ACT, AX = mybir.AluOpType, mybir.ActivationFunctionType, mybir.AxisListType


def wait(eng, sem, value):
    if not isinstance(value, int) or value > 0:
        eng.wait_ge(sem, value)


class Count:

    def __init__(self, eng, sem, per, n):
        self.eng, self.sem, self.per, self.base, self.k = eng, sem, per, per * n, 0

    def __call__(self, ins):
        ins.then_inc(self.sem, 1)
        self.k += 1

    def wait(self):
        wait(self.eng, self.sem, self.base + self.k)

    def end(self):
        assert self.k == self.per, (self.k, self.per)


def tower(nc, x, emb2, emb3, emb4, w1, w3, w2, sw1, sw3, sw2, proj_t, qkv_t, out_t, gate_t,
          bias_rows, bias_cols, pre_cols, post_row, rope, consts, iotas, ids, out):
    with ExitStack() as ctx:
        def sb(name, shape, dt=f32):
            return ctx.enter_context(nc.sbuf_tensor(name, shape, dt))

        def sem(name):
            return ctx.enter_context(nc.semaphore(name))

        lists = nc.dram_tensor("lists", [DUMMY + P, ROW], f32).ap()
        acc = [nc.dram_tensor(f"acc{r}", [CAP, D], f32).ap() for r in range(ACCS)]

        w13_sb = sb("w13_sb", [P, E, 2 * IE])
        w2_sb = sb("w2_sb", [P, E, D])
        sw1_sb = sb("sw1_sb", [P, IS])
        sw3_sb = sb("sw3_sb", [P, IS])
        sw2_sb = sb("sw2_sb", [P, 3, D])
        proj_sb = sb("proj_sb", [P, NGRAMS, D])
        qkv_sb = sb("qkv_sb", [P, 5, D])
        outw_sb = sb("outw_sb", [P, D])
        gate_sb = sb("gate_sb", [P, E])
        brow = sb("brow", [1, 3, D])
        bcol = sb("bcol", [P, 4])
        pre_sb = sb("pre_sb", [P, NH])
        npre = sb("npre", [P, NH])
        post_sb = sb("post_sb", [P, NH, D])
        rope_sb = sb("rope_sb", [P, 2, S])
        const_sb = sb("const_sb", [P, 3 * P + E + ROW])
        ident, ones = const_sb[:, 0:P], const_sb[:, P:2 * P]
        before = const_sb[:, 2 * P:3 * P]
        base1 = const_sb[:, 3 * P:3 * P + E]
        pad = const_sb[:, 3 * P + E:3 * P + E + ROW]
        iota_sb = sb("iota_sb", [E, TILES + 16 + E])
        tile_no, tile_lo = iota_sb[:, 0:TILES], iota_sb[:, TILES:TILES + 16]
        upto = iota_sb[:, TILES + 16:TILES + 16 + E]
        ids_sb = sb("ids_sb", [P, NT], i32)
        ones_h = sb("ones_h", [P, P], bf16)
        before_h = sb("before_h", [P, P], bf16)

        xi = sb("xi", [B, S], i32)
        xf = sb("xf", [B, S + 4])
        hash_f = sb("hash_f", [B, NGRAMS, S + 1])
        quo = sb("quo", [B, S + 1], i32)
        quo_f = sb("quo_f", [B, S + 1])
        fix = sb("fix", [B, S + 1])
        idx_all = sb("idx_all", [P, B + 1, TPS * NGRAMS], i32)
        idx_cur = sb("idx_cur", [P, TPS * NGRAMS], i32)

        emb_g = sb("emb_g", [P, TPS * NGRAMS, D])
        emb_t = sb("emb_t", [P, NGRAMS, S])
        h_all = sb("h_all", [P, NT, D])
        stat = sb("stat", [P, 2, TPS, 6])
        mv = sb("mv", [P, 2, TPS, 2])
        nt = sb("nt", [P, 2, 3, TPS])
        xn = sb("xn", [P, TPS, D])
        xn_t = sb("xn_t", [P, S])
        rt = sb("rt", [P, 2, S])
        q_sb = sb("q_sb", [P, 2, S])
        k_sb = sb("k_sb", [P, 2, S])
        v_sb = sb("v_sb", [P, 2, TPS, D])

        qh = sb("qh", [P, 2, S])
        vh = sb("vh", [P, 4, TPS, D])
        neg_max = sb("neg_max", [P, 4, TPS])
        total = sb("total", [P, 4, TPS])
        inv = sb("inv", [P, 4, TPS])
        pr = sb("pr", [P, 4, TPS, S])
        pr_t = sb("pr_t", [P, 2, 2 * S])

        o_t = sb("o_t", [P, S])
        row = sb("row", [P, 2, TPS, ROW])
        xn2_cur = sb("xn2_cur", [P, S])
        xn2_t = sb("xn2_t", [P, T])
        top = sb("top", [P, TPS, 8])
        left = sb("left", [P, TPS, E])
        mask = sb("mask", [P, TPS, E], bf16)
        ntop = sb("ntop", [P, TPS])
        ex = sb("ex", [P, TPS, E])
        wsum = sb("wsum", [P, 2, TPS])
        cum = sb("cum", [P, E], bf16)
        posm = sb("posm", [P, TPS, E])
        pos8 = sb("pos8", [P, TPS, 8])
        pos = sb("pos", [P, 2, TPS, 8], i32)

        cnt = sb("cnt", [E, 1])
        ntiles = sb("ntiles", [E, 1])
        ends = sb("ends", [E, 1])
        gap = sb("gap", [E, 1])
        cmp16 = sb("cmp16", [E, 16])
        past = sb("past", [E, TILES])
        tab_e = sb("tab_e", [1, TILES + 4], i32)
        tab_off = sb("tab_off", [1, TILES], i32)
        offf = sb("offf", [1, TILES])
        tab_pad = sb("tab_pad", [1, E], i32)

        rows = sb("rows", [P, RING, ROW])
        x_t = sb("x_t", [P, 2, 2, P])
        sg = sb("sg", [P, 2, 2, IE])
        hid = sb("hid", [P, 2, 2, IE])
        hid_t = sb("hid_t", [P, 2, 2, P])
        y_sb = xn2_t[:, :].rearrange("p (r d) -> p r d", r=RING)
        sh_g = pr[:, 0, :, :].rearrange("p a s -> p (a s)")
        sh_hid = pr[:, 1:4, :, :].rearrange("p m a s -> p m (a s)")
        acc_in = w13_sb[:, :, :].rearrange("p e n -> p (e n)")[:, 0:ACCS * NT * D] \
            .rearrange("p (r t d) -> p r t d", r=ACCS, t=NT)

        ps = ctx.enter_context(nc.psum_tensor("ps", [P, 8, 512], f32))
        SC, PT, OB, M0, M1, M2 = (0, 1), (2, 3), 4, 5, 6, 7

        L = sem("loaded_x"); LC = sem("loaded_consts"); LW = sem("loaded_experts"); LS = sem("loaded_shared")
        zeroed = sem("accumulators_zeroed")
        setup = sem("setup_done"); hashed = sem("hash_step"); hash_t = sem("hash_transposed"); idx_ok = sem("indices_ready")
        idx_n = sem("indices_of_sequence"); gathered = sem("rows_gathered")
        e_tr = sem("emb_transposed"); e_ev = sem("emb_evacuated"); e_zero = sem("emb_edges_zeroed")
        e_proj = sem("projected"); ln1 = sem("norm1_step"); e_xt = sem("norm1_transposed"); e_xe = sem("norm1_evacuated")
        v_mm = sem("v_product"); q_mm = sem("q_product"); k_mm = sem("k_product")
        v_ev = sem("v_ready"); q_rp = sem("q_rope_step"); k_rp = sem("k_rope_step")
        prep = sem("head_operands"); sc_mm = sem("scores"); mx = sem("score_max"); exd = sem("exponentials")
        nrm = sem("norm_step"); p_tr = sem("probs_transposed"); p_ev = sem("probs_evacuated"); pv = sem("values_summed")
        o_ev = sem("attended_evacuated"); o_mm = sem("attended_projected"); ln2 = sem("norm2_step")
        r_xt = sem("norm2_transposed"); r_xe = sem("norm2_evacuated"); g_mm = sem("gate_scores")
        tk = sem("topk_step"); g_ex = sem("gate_exponentials"); rk_mm = sem("ranks"); ps_s = sem("position_step")
        sent = [sem("rows_sent_even"), sem("rows_sent_odd")]; row_free = sem("row_buffer_free")
        c_mm = sem("counts"); tb = sem("table_step"); padded = sem("padding_written")
        shg = sem("shared_products"); sha = sem("shared_silu"); shh = sem("shared_hidden"); shy = sem("shared_out"); she = sem("shared_added")
        x_ld = [sem(f"pair_loaded{k}") for k in range(PAIRS)]
        x_tr = sem("tile_transposed"); x_ev = sem("tile_evacuated"); h_mm = sem("hidden_product"); h_si = sem("silu_done")
        h_mu = sem("hidden_ready"); h_tr = sem("hidden_transposed"); h_ev = sem("hidden_evacuated"); y_mm = sem("expert_out")
        y_ev = sem("weighted_out"); added = [sem(f"scattered{r}") for r in range(ACCS)]
        acc_ld = sem("accumulators_loaded"); fin = sem("final_step"); stored = sem("stored"); passed = sem("wait_passed")
        block = ctx.enter_context(nc.Block())

        N_SETUP, N_HASH, N_LN1, N_LN2, N_TK, N_PS = 5, 20, 19, 20, 11, 7

        def hold(eng, sem_, value):
            if not isinstance(value, int) or value > 0:
                eng.wait_ge(sem_, value)
                eng.sem_inc(passed, 1)

        def front(eng, slot):
            for s in range(NH):
                slot(0, 0, s, True, False)
            with eng.Fori(0, 3) as j:
                for par in (1, 0):
                    for s in range(NH):
                        slot(2 * j + (1 if par else 2), par, s, True, True)
            for s in range(NH):
                slot(B - 1, 1, s, False, True)

        def table(ap, engine, most):
            return nc.values_load_multi_w_load_instructions(
                ap, engines=[engine], min_val=0, max_val=most,
                skip_runtime_bounds_check_because="the tables' entries are clamped where they are made")[1]

        def write_padding(eng, nce, engine, first):
            with nce.Fori(0, 2) as g:
                at = table(tab_pad[0:1, bass.ds(16 * g + first, 16)], engine, DUMMY - P)
                for a in at:
                    eng.dma_start(lists[bass.ds(a, P), :], pad).then_inc(padded, 16)

        @block.sync
        def _(sp):
            sp.dma_start(xi[:, :], x).then_inc(L, 16)
            for dst, src in ((const_sb[:, :], consts), (iota_sb[:, :], iotas), (ids_sb[:, :], ids),
                             (proj_sb[:, :, :], proj_t.rearrange("(g p) d -> p g d", p=P)),
                             (qkv_sb[:, :, :], qkv_t.rearrange("p (a d) -> p a d", a=5)),
                             (brow[:, :, :], bias_rows.rearrange("(o a) d -> o a d", o=1)), (bcol[:, :], bias_cols),
                             (pre_sb[:, :], pre_cols), (rope_sb[:, :, :], rope.rearrange("a p s -> p a s")),
                             (post_sb[:, :, :], post_row.to_broadcast([P, NH, D])),
                             (outw_sb[:, :], out_t), (gate_sb[:, :], gate_t)):
                sp.dma_start(dst, src).then_inc(LC, 16)
            for dst, src in ((sw1_sb[:, :], sw1), (sw3_sb[:, :], sw3),
                             (sw2_sb[:, 0:2, :], sw2[0:2 * P, :].rearrange("(m p) d -> p m d", p=P)),
                             (sw2_sb[0:IS - 2 * P, 2, :], sw2[2 * P:IS, :])):
                sp.dma_start(dst, src).then_inc(LS, 16)
            sp.wait_ge(LC, 16 * 12)
            for c in range(B):
                sp.wait_ge(gathered, 16 * TPS * NGRAMS * (c + 1))
                e = slice(E // B * c, E // B * (c + 1))
                sp.dma_start(w13_sb[:, e, 0:IE], w1[e].rearrange("e h i -> h e i")).then_inc(LW, 16)
                sp.dma_start(w13_sb[:, e, IE:2 * IE], w3[e].rearrange("e h i -> h e i")).then_inc(LW, 16)
                sp.dma_start(w2_sb[:, e, :], w2[e].rearrange("e i h -> i e h")).then_inc(LW, 16)
                if c >= B - ACCS:
                    sp.dma_start(acc[c - B + ACCS].rearrange("(a p) d -> p a d", p=P),
                                 pad[:, 0:D].rearrange("p (o d) -> p o d", o=1).to_broadcast([P, CAP // P, D])).then_inc(zeroed, 16)
            sp.dma_start(lists[DUMMY:DUMMY + P, :], pad).then_inc(padded, 16)
            sp.wait_ge(tb, 8)
            write_padding(sp, nc.sync, mybir.EngineType.SP, 0)
            sp.wait_ge(padded, 16 * (E + 1))
            for par in range(2):
                sp.wait_ge(sent[par], 16 * TPS * K * (B // 2))
            sp.wait_ge(tb, 12)

            def group(j, first):
                at = table(tab_off[0:1, bass.ds(RING * j, RING)], mybir.EngineType.SP, DUMMY)
                for r in range(RING):
                    if not first:
                        sp.wait_ge(added[r % ACCS], 16 * (PER_ACC * (j - 1) + r // ACCS + 1))
                    sp.dma_start(rows[:, r, :], lists[bass.ds(at[r], P), :]).then_inc(x_ld[r // 2], 16)

            group(0, True)
            with nc.sync.Fori(1, GROUPS) as j:
                group(j, False)
            for r in range(ACCS):
                sp.wait_ge(added[r], 16 * (TILES // ACCS))
                sp.dma_start(acc_in[:, r, :, :], acc[r][0:T, :].rearrange("(t p) d -> p t d", p=P)).then_inc(acc_ld, 16)
            for g in range(4):
                t = slice(4 * g, 4 * g + 4)
                sp.wait_ge(fin, ACCS * (g + 1))
                sp.dma_start(out.rearrange("b (c p) d -> p (b c) d", p=P)[:, t, :], h_all[:, t, :]).then_inc(stored, 16)
            sp.wait_ge(stored, 16 * 4)

        @block.gpsimd
        def _(pool):
            tables = (emb2, emb3, emb4)

            def gather(n):
                hold(pool, idx_n, n + 1)
                if not isinstance(n, int) or n > 0:
                    hold(pool, e_tr, TPS * n)
                for a in range(TPS * NGRAMS):
                    nc.gpsimd.indirect_dma_start(
                        out=emb_g[:, a, :], out_offset=None, in_=tables[a % NGRAMS],
                        in_offset=bass.IndirectOffsetOnAxis(ap=idx_cur[:, a:a + 1], axis=0)).then_inc(gathered, 16)

            def send(n, par):
                hold(pool, ps_s, N_PS * (n + 1))
                for it in range(TPS):
                    for c in range(K):
                        nc.gpsimd.indirect_dma_start(
                            out=lists, out_offset=bass.IndirectOffsetOnAxis(ap=pos[:, par, it, c:c + 1], axis=0),
                            in_=row[:, par, it, :], in_offset=None).then_inc(sent[par], 16)

            def free_rows(m):
                pool.wait_ge(sent[(m - 1) % 2] if isinstance(m, int) else m[0], 16 * TPS * K * ((m - 1) // 2 + 1 if isinstance(m, int) else m[1]))
                pool.sem_inc(row_free, 1)

            pool.sem_inc(row_free, 2)
            gather(0)
            gather(1)
            gather(2)
            gather(3)
            send(0, 0)
            with nc.gpsimd.Fori(0, 2) as j:
                gather(2 * j + 4)
                free_rows((sent[0], j + 1))
                send(2 * j + 1, 1)
                gather(2 * j + 5)
                free_rows((sent[1], j + 1))
                send(2 * j + 2, 0)
            for m in (5, 6, 7):
                free_rows(m)
                send(m, m % 2)
            pool.wait_ge(zeroed, 16 * ACCS)


            def group(j, first):
                for r in range(RING):
                    pool.wait_ge(y_ev, RING * j + r + 1)
                    if not (first and r < ACCS):
                        pool.wait_ge(added[r % ACCS], 16 * (PER_ACC * j + r // ACCS))
                    pool.sem_inc(passed, 1)
                    nc.gpsimd.indirect_dma_start(
                        out=acc[r % ACCS], out_offset=bass.IndirectOffsetOnAxis(ap=rows[:, r, ROW - 1:ROW].bitcast(i32), axis=0),
                        in_=y_sb[:, r, :], in_offset=None, compute_op=ALU.add).then_inc(added[r % ACCS], 16)

            group(0, True)
            with nc.gpsimd.Fori(1, GROUPS) as j:
                group(j, False)

        @block.tensor
        def _(pe):
            mm = nc.tensor.matmul

            def embed_transpose(n):
                wait(pe, gathered, 16 * TPS * NGRAMS * (n + 1))
                wait(pe, k_rp, 3 * n)
                wait(pe, q_rp, 3 * n)
                for it in range(TPS):
                    for g in range(NGRAMS):
                        last = nc.tensor.transpose(ps[:, (M0, M1)[it], g * P:(g + 1) * P], emb_g[:, it * NGRAMS + g, :], ident)
                    last.then_inc(e_tr, 1)

            def project(n):
                wait(pe, e_zero, 3 * (n + 1))
                for it in range(TPS):
                    o = ps[:, M0, it * P:(it + 1) * P]
                    for g in range(NGRAMS):
                        mm(o, lhsT=emb_t[:, g, it * P:(it + 1) * P], rhs=proj_sb[:, g, :], start=(g == 0), stop=False)
                    last = mm(o, lhsT=ones[0:1, :], rhs=brow[0:1, 0, :], start=False, stop=True)
                last.then_inc(e_proj, 1)

            def norm1_transpose(n):
                wait(pe, ln1, N_LN1 * (n + 1))
                for it in range(TPS):
                    last = nc.tensor.transpose(ps[:, M1, it * P:(it + 1) * P], xn[:, it, :], ident)
                last.then_inc(e_xt, 1)

            def make_vq(n):
                wait(pe, e_xe, n + 1)
                for it in range(TPS):
                    o = ps[:, M0, it * P:(it + 1) * P]
                    mm(o, lhsT=xn_t[:, it * P:(it + 1) * P], rhs=qkv_sb[:, 4, :], start=True, stop=False)
                    last = mm(o, lhsT=ones[0:1, :], rhs=brow[0:1, 1, :], start=False, stop=True)
                last.then_inc(v_mm, 1)
                for a in range(2):
                    last = mm(ps[:, M1, a * S:(a + 1) * S], lhsT=qkv_sb[:, a, :], rhs=xn_t[:, :], start=True, stop=True)
                last.then_inc(q_mm, 1)

            def make_k(n):
                wait(pe, v_ev, n + 1)
                for a in range(2):
                    last = mm(ps[:, M0, a * S:(a + 1) * S], lhsT=qkv_sb[:, 2 + a, :], rhs=xn_t[:, :], start=True, stop=True)
                last.then_inc(k_mm, 1)

            def scores(b, par, h):
                wait(pe, prep, 2 * (NH * b + h + 1))
                wait(pe, exd, 2 * (NH * b + h - 1))
                for it in range(TPS):
                    last = mm(ps[:, SC[h % 2], it * S:(it + 1) * S], lhsT=qh[:, h % 2, it * P:(it + 1) * P],
                              rhs=k_sb[:, par, :], start=True, stop=True)
                last.then_inc(sc_mm, 1)

            def probs_transpose(u, h):
                wait(pe, nrm, 3 * (u + 1))
                wait(pe, p_ev, u - 1)
                for jt in range(2):
                    for it in range(TPS):
                        last = nc.tensor.transpose(ps[:, PT[h % 2], jt * S + it * P:jt * S + (it + 1) * P],
                                                   pr[:, h % 4, it, jt * P:(jt + 1) * P], ident)
                last.then_inc(p_tr, 1)

            def values(u, b, h):
                wait(pe, p_ev, u + 1)
                if h == 0:
                    wait(pe, o_ev, b)
                for jt in range(2):
                    last = mm(ps[:, OB, 0:S], lhsT=vh[:, h % 4, jt, :], rhs=pr_t[:, h % 2, jt * S:(jt + 1) * S],
                              start=(h == 0 and jt == 0), stop=(h == NH - 1 and jt == 1))
                last.then_inc(pv, 1)

            def out_project(n):
                wait(pe, o_ev, n + 1)
                for it in range(TPS):
                    o = ps[:, M2, it * P:(it + 1) * P]
                    mm(o, lhsT=o_t[:, it * P:(it + 1) * P], rhs=outw_sb[:, :], start=True, stop=False)
                    last = mm(o, lhsT=ones[0:1, :], rhs=brow[0:1, 2, :], start=False, stop=True)
                last.then_inc(o_mm, 1)

            def norm2_transpose(n, par):
                wait(pe, ln2, N_LN2 * (n + 1))
                for it in range(TPS):
                    last = nc.tensor.transpose(ps[:, M2, it * P:(it + 1) * P], row[:, par, it, 0:D], ident)
                last.then_inc(r_xt, 1)

            def gate(n):
                wait(pe, r_xe, n + 1)
                for it in range(TPS):
                    last = mm(ps[:, M2, it * E:(it + 1) * E], lhsT=xn2_cur[:, it * P:(it + 1) * P], rhs=gate_sb[:, :],
                              start=True, stop=True)
                last.then_inc(g_mm, 1)

            def rank(n):
                wait(pe, tk, N_TK * (n + 1))
                for it in range(TPS):
                    o = ps[:, M2, 128 + it * E:128 + (it + 1) * E]
                    mm(o, lhsT=before_h[:, :], rhs=mask[:, it, :], start=True, stop=False)
                    if it:
                        mm(o, lhsT=ones_h[:, :], rhs=mask[:, 0, :], start=False, stop=False)
                    last = mm(o, lhsT=ones_h[:, :], rhs=cum[:, :], start=False, stop=True)
                last.then_inc(rk_mm, 1)

            pe.wait_ge(LC, 16 * 12)
            pe.wait_ge(hashed, N_HASH)
            for it in range(TPS):
                for g in range(NGRAMS):
                    o = ps[:, M2, 0:B * TPS * NGRAMS].rearrange("p (b a) -> p b a", b=B)[:, :, it * NGRAMS + g]
                    s0 = it * P + (1 if g < 2 else 0)
                    last = mm(o, lhsT=hash_f[:, g, s0:s0 + P], rhs=ident[0:B, 0:B], start=True, stop=True)
            last.then_inc(hash_t, 1)
            pe.wait_ge(setup, N_SETUP)
            embed_transpose(0)
            project(0)
            norm1_transpose(0)
            make_vq(0)
            make_k(0)

            def slot(b, par, s, embeds, routes):
                scores(b, par, s)
                u = NH * b + s
                if routes or s >= 2:
                    probs_transpose(u - 2, (s - 2) % NH)
                if routes or s >= 3:
                    values(u - 3, b if s >= 3 else b - 1, (s - 3) % NH)
                if embeds and s == 0:
                    embed_transpose(b + 1)
                if embeds and s == 1:
                    project(b + 1)
                if embeds and s == 3:
                    norm1_transpose(b + 1)
                if routes and s == 3:
                    out_project(b - 1)
                if embeds and s == 4:
                    make_vq(b + 1)
                if embeds and s == 5:
                    make_k(b + 1)
                if routes and s == 5:
                    norm2_transpose(b - 1, 1 - par)
                if routes and s == 6:
                    gate(b - 1)
                if routes and s == 7:
                    rank(b - 1)

            front(nc.tensor, slot)
            U = NH * B
            probs_transpose(U - 2, 6)
            values(U - 3, B - 1, 5)
            probs_transpose(U - 1, 7)
            values(U - 2, B - 1, 6)
            values(U - 1, B - 1, 7)
            out_project(B - 1)
            norm2_transpose(B - 1, 1)
            gate(B - 1)
            rank(B - 1)

            pe.wait_ge(ps_s, N_PS * B)
            mm(ps[0:E, M0, 0:1], lhsT=cum[:, :], rhs=ones_h[:, 0:1], start=True, stop=True)
            mm(ps[0:1, M1, 0:E], lhsT=ones_h[:, 0:1], rhs=cum[:, :], start=True, stop=True).then_inc(c_mm, 1)
            pe.wait_ge(tb, 4)
            mm(ps[0:E, M2, 0:1], lhsT=upto, rhs=ntiles[:, :], start=True, stop=True).then_inc(c_mm, 1)
            pe.wait_ge(tb, 9)
            mm(ps[0:1, M0, 0:TILES], lhsT=ones[0:E, 0:1], rhs=past[:, :], start=True, stop=True)
            mm(ps[0:1, M1, 0:TILES], lhsT=gap[:, :], rhs=past[:, :], start=True, stop=True).then_inc(c_mm, 1)

            pe.wait_ge(LS, 16 * 4)
            pe.wait_ge(r_xe, B)
            def shared(c):
                for m, (lo, w) in enumerate(SHM):
                    k = 3 * c + m
                    wait(pe, shh, k - 1)
                    for a, wt in enumerate((sw1_sb, sw3_sb)):
                        last = mm(ps[0:w, 2 * (m % 2) + a, :], lhsT=wt[:, lo:lo + w], rhs=xn2_t[:, bass.ds(c * SHC, SHC)],
                                  start=True, stop=True)
                    last.then_inc(shg, 1)
                    if m == 1:
                        wait(pe, shh, k)
                wait(pe, shh, 3 * c + 3)
                wait(pe, she, c)
                for t in range(SHC // P):
                    for m, (lo, w) in enumerate(SHM):
                        last = mm(ps[:, OB, t * P:(t + 1) * P], lhsT=sh_hid[0:w, m, t * P:(t + 1) * P], rhs=sw2_sb[0:w, m, :],
                                  start=(m == 0), stop=(m == 2))
                last.then_inc(shy, 1)

            for c in range(T // SHC):
                shared(c)
            pe.wait_ge(she, T // SHC)

            pe.wait_ge(LW, 16 * 24)
            pe.wait_ge(tb, 12)


            def tile_transpose(q, k, j):
                wait(pe, x_ld[k], 32 * (j + 1))
                wait(pe, x_ev, q - 1)
                for t in range(2):
                    last = nc.tensor.transpose(ps[:, k % 2, t * P:(t + 1) * P], rows[:, 2 * k + t, 0:D], ident)
                last.then_inc(x_tr, 1)

            def hidden(q, k, e):
                wait(pe, x_ev, q + 1)
                wait(pe, h_mu, q - 1)
                for t in range(2):
                    last = mm(ps[:, 2 + k % 2, t * 2 * IE:(t + 1) * 2 * IE], lhsT=x_t[:, k % 2, t, :],
                              rhs=w13_sb[:, bass.ds(e[t], 1), :].rearrange("p a n -> p (a n)"), start=True, stop=True)
                last.then_inc(h_mm, 1)

            def hidden_transpose(q, k):
                wait(pe, h_mu, q + 1)
                wait(pe, h_ev, q - 1)
                for t in range(2):
                    last = nc.tensor.transpose(ps[:, 4 + k % 2, t * P:(t + 1) * P], hid[:, k % 2, t, :], ident)
                last.then_inc(h_tr, 1)

            def down(q, k, e):
                wait(pe, h_ev, q + 1)
                wait(pe, y_ev, 2 * (q - 1))
                for t in range(2):
                    last = mm(ps[:, 6 + k % 2, t * D:(t + 1) * D], lhsT=hid_t[:, k % 2, t, :],
                              rhs=w2_sb[:, bass.ds(e[t], 1), :].rearrange("p a n -> p (a n)"), start=True, stop=True)
                last.then_inc(y_mm, 1)

            def group(j, first, last):
                q = PAIRS * j
                n = RING + (2 if last else 4)
                e = table(tab_e[0:1, bass.ds(RING * j, n)], mybir.EngineType.PE, E - 1)
                if first:
                    tile_transpose(0, 0, 0)
                    tile_transpose(1, 1, 0)
                    hidden(0, 0, e[2:4])
                for k in range(PAIRS):
                    if not (last and k >= PAIRS - 2):
                        tile_transpose(q + k + 2, (k + 2) % PAIRS, j + (k + 2) // PAIRS)
                    if not (last and k == PAIRS - 1):
                        hidden(q + k + 1, (k + 1) % PAIRS, e[2 * k + 4:2 * k + 6])
                    hidden_transpose(q + k, k)
                    if not (first and k == 0):
                        down(q + k - 1, (k - 1) % PAIRS, e[2 * k:2 * k + 2])
                if last:
                    down(q + PAIRS - 1, PAIRS - 1, e[RING:RING + 2])

            group(0, True, False)
            with nc.tensor.Fori(1, GROUPS - 1) as j:
                group(j, False, False)
            group(GROUPS - 1, False, True)

        @block.scalar
        def _(act):
            copy = ACT.Copy

            def embed_evac(n):
                for it in range(TPS):
                    wait(act, e_tr, TPS * n + it + 1)
                    if it == 0:
                        wait(act, e_proj, n)
                    nc.scalar.activation(emb_t[:, :, it * P:(it + 1) * P],
                                         ps[:, (M0, M1)[it], 0:NGRAMS * P].rearrange("p (g t) -> p g t", g=NGRAMS), copy).then_inc(e_ev, 1)

            def norm1_evac(n):
                wait(act, e_xt, n + 1)
                wait(act, k_mm, n)
                nc.scalar.activation(xn_t[:, :], ps[:, M1, 0:S], copy).then_inc(e_xe, 1)

            def exps(u, h):
                wait(act, mx, u + 1)
                wait(act, p_tr, u - 3)
                for it in range(TPS):
                    nc.scalar.activation(pr[:, h % 4, it, :], ps[:, SC[h % 2], it * S:(it + 1) * S], ACT.Exp,
                                         bias=neg_max[:, h % 4, it:it + 1], scale=-1.0,
                                         accum_out=total[:, h % 4, it:it + 1]).then_inc(exd, 1)

            def probs_evac(u, h):
                wait(act, p_tr, u + 1)
                wait(act, pv, u - 1)
                nc.scalar.activation(pr_t[:, h % 2, :], ps[:, PT[h % 2], :], copy).then_inc(p_ev, 1)

            def attended_evac(n):
                wait(act, pv, NH * (n + 1))
                nc.scalar.activation(o_t[:, :], ps[:, OB, 0:S], copy).then_inc(o_ev, 1)

            def norm2_evac(n):
                wait(act, r_xt, n + 1)
                nc.scalar.activation(xn2_t[:, bass.ds(n * S, S)], ps[:, M2, 0:S], copy)
                nc.scalar.activation(xn2_cur[:, :], ps[:, M2, 0:S], copy).then_inc(r_xe, 1)

            def gate_exps(n):
                wait(act, tk, N_TK * n + 6)
                for it in range(TPS):
                    nc.scalar.activation(ex[:, it, :], ps[:, M2, it * E:(it + 1) * E], ACT.Exp,
                                         bias=ntop[:, it:it + 1], scale=1.0).then_inc(g_ex, 1)

            embed_evac(0)
            norm1_evac(0)

            def slot(b, par, s, embeds, routes):
                u = NH * b + s
                exps(u, s)
                if routes or s >= 2:
                    probs_evac(u - 2, (s - 2) % NH)
                if embeds and s == 0:
                    embed_evac(b + 1)
                if embeds and s == 3:
                    norm1_evac(b + 1)
                if routes and s == 2:
                    attended_evac(b - 1)
                if routes and s == 5:
                    norm2_evac(b - 1)
                if routes and s == 6:
                    gate_exps(b - 1)

            front(nc.scalar, slot)
            U = NH * B
            probs_evac(U - 2, 6)
            probs_evac(U - 1, 7)
            attended_evac(B - 1)
            norm2_evac(B - 1)
            gate_exps(B - 1)

            act.wait_ge(tb, 8)
            write_padding(act, nc.scalar, mybir.EngineType.Activation, E // 2)

            for c in range(T // SHC):
                for m, (lo, w) in enumerate(SHM):
                    wait(act, shg, 3 * c + m + 1)
                    wait(act, shh, 3 * c + m)
                    nc.scalar.activation(sh_g[0:w, :], ps[0:w, 2 * (m % 2), :], ACT.Silu).then_inc(sha, 1)

            def silu(q, k):
                wait(act, h_mm, q + 1)
                wait(act, h_mu, q - 1)
                nc.scalar.activation(sg[:, k % 2, :, :], ps[:, 2 + k % 2, :].rearrange("p (t a n) -> p t a n", t=2, a=2)[:, :, 0, :],
                                     ACT.Silu).then_inc(h_si, 1)

            def hid_evac(q, k):
                wait(act, h_tr, q + 1)
                wait(act, y_mm, q - 1)
                nc.scalar.activation(hid_t[:, k % 2, :, :].rearrange("p t n -> p (t n)"), ps[:, 4 + k % 2, 0:2 * P], copy).then_inc(h_ev, 1)

            def group(j, last):
                for k in range(PAIRS):
                    if not (last and k == PAIRS - 1):
                        silu(PAIRS * j + k + 1, (k + 1) % PAIRS)
                    hid_evac(PAIRS * j + k, k)

            silu(0, 0)
            group(0, False)
            with nc.scalar.Fori(1, GROUPS - 1) as j:
                group(j, False)
            group(GROUPS - 1, True)

        @block.vector
        def _(dve):
            v = nc.vector

            def rsqrt(st, n, which):
                var, y, a = nt[:, which, 0, :], nt[:, which, 1, :], nt[:, which, 2, :]
                st.wait()
                st(v.tensor_scalar(var, mv[:, which, :, 1], 1e-5, None, ALU.add))
                st.wait()
                st(v.tensor_scalar(a.bitcast(i32), var.bitcast(i32), 1, None, ALU.arith_shift_right))
                st.wait()
                st(v.tensor_scalar(y.bitcast(i32), a.bitcast(i32), -1.0, float(0x5F3759DF), ALU.mult, ALU.add))
                for _ in range(3):
                    st.wait()
                    st(v.tensor_tensor(a, y, y, ALU.mult))
                    st.wait()
                    st(v.scalar_tensor_tensor(out=a, in0=a, scalar=-0.5, in1=var, op0=ALU.mult, op1=ALU.mult))
                    st.wait()
                    st(v.scalar_tensor_tensor(out=y, in0=a, scalar=1.5, in1=y, op0=ALU.add, op1=ALU.mult))
                st.wait()

            def indices(n):
                if not isinstance(n, int) or n > 0:
                    wait(dve, gathered, 16 * TPS * NGRAMS * n)
                    v.tensor_scalar(idx_cur[:, :], idx_all[:, bass.ds(n, 1), :].rearrange("p o a -> p (o a)"), 0, None, ALU.add).then_inc(idx_n, 1)
                else:
                    v.tensor_copy(idx_cur[:, :], idx_all[:, 0, :]).then_inc(idx_n, 1)

            def edges(n):
                wait(dve, e_ev, TPS * (n + 1))
                v.memset(emb_t[:, 0:3, 0:1], 0.0).then_inc(e_zero, 1)
                v.memset(emb_t[:, 1:3, S - 1:S], 0.0).then_inc(e_zero, 1)
                v.memset(emb_t[:, 2:3, 1:2], 0.0).then_inc(e_zero, 1)

            def norm1(n):
                st = Count(dve, ln1, N_LN1, n)
                wait(dve, e_proj, n + 1)
                wait(dve, e_xt, n)
                src = ps[:, M0, 0:TPS * D].rearrange("p (t d) -> p t d", t=TPS)
                st(v.tensor_scalar(h_all[:, bass.ds(TPS * n, TPS), :], src, 0.0, None, ALU.add))
                for it in range(TPS):
                    st(v.bn_stats(stat[:, 0, it, :], src[:, it, :]))
                hold(dve, ln1, st.base + st.k)
                for it in range(TPS):
                    st(v.bn_aggr(mv[:, 0, it, :], stat[:, 0, it, :]))
                rsqrt(st, n, 0)
                for it in range(TPS):
                    st(v.tensor_scalar(xn[:, it, :], src[:, it, :], mv[:, 0, it, 0:1], nt[:, 0, 1, it:it + 1], ALU.subtract, ALU.mult))
                st.end()

            def evac_v(n, par):
                wait(dve, v_mm, n + 1)
                wait(dve, prep, 2 * NH * (n - 1))
                v.tensor_scalar(v_sb[:, par, :, :].rearrange("p t d -> p (t d)"), ps[:, M0, 0:TPS * D], 0.0, None, ALU.add).then_inc(v_ev, 1)

            def rotate(n, par, src_sem, sem_, bank, dst, col):
                st = Count(dve, sem_, 3, n)
                wait(dve, src_sem, n + 1)
                if dst is q_sb:
                    wait(dve, k_rp, 3 * n)
                else:
                    wait(dve, q_rp, 3 * (n + 1))
                    wait(dve, sc_mm, NH * (n - 1))
                for a in range(2):
                    st(v.scalar_tensor_tensor(out=rt[:, a, :], in0=ps[:, bank, a * S:(a + 1) * S], scalar=bcol[:, col + a:col + a + 1],
                                              in1=rope_sb[:, a, :], op0=ALU.add, op1=ALU.mult))
                st.wait()
                st(v.tensor_tensor(dst[:, par, :], rt[:, 0, :], rt[:, 1, :], ALU.add))
                st.end()

            def prepare(b, par, h):
                u = NH * b + h
                wait(dve, k_rp, 3 * (b + 1))
                wait(dve, q_rp, 3 * (b + 1))
                wait(dve, v_ev, b + 1)
                wait(dve, sc_mm, u - 1)
                wait(dve, pv, u - 3)
                v.tensor_scalar(qh[:, h % 2, :], q_sb[:, par, :], npre[:, h:h + 1], None, ALU.mult).then_inc(prep, 1)
                v.tensor_tensor(vh[:, h % 4, :, :], v_sb[:, par, :, :],
                                post_sb[:, h:h + 1, :].to_broadcast([P, TPS, D]), ALU.mult).then_inc(prep, 1)

            def maxima(u, h):
                wait(dve, sc_mm, u + 1)
                wait(dve, exd, 2 * (u - 3))
                v.tensor_reduce(neg_max[:, h % 4, :], ps[:, SC[h % 2], :].rearrange("p (t s) -> p t s", t=TPS), AX.X, ALU.min).then_inc(mx, 1)

            def normalise(u, h):
                wait(dve, exd, 2 * (u + 1))
                v.reciprocal(inv[:, h % 4, :], total[:, h % 4, :]).then_inc(nrm, 1)
                wait(dve, nrm, 3 * u + 1)
                for it in range(TPS):
                    v.tensor_scalar(pr[:, h % 4, it, :], pr[:, h % 4, it, :], inv[:, h % 4, it:it + 1], None, ALU.mult).then_inc(nrm, 1)

            def residual_norm2(n, par):
                st = Count(dve, ln2, N_LN2, n)
                hs = h_all[:, bass.ds(TPS * n, TPS), :]
                wait(dve, o_mm, n + 1)
                wait(dve, ln1, N_LN1 * (n + 1))
                wait(dve, row_free, n + 1)
                st(v.tensor_tensor(hs, ps[:, M2, 0:TPS * D].rearrange("p (t d) -> p t d", t=TPS), hs, ALU.add))
                hold(dve, ln2, st.base + st.k)
                for it in range(TPS):
                    st(v.bn_stats(stat[:, 1, it, :], h_all[:, bass.ds(TPS * n + it, 1), :].rearrange("p o d -> p (o d)")))
                hold(dve, ln2, st.base + st.k)
                for it in range(TPS):
                    st(v.bn_aggr(mv[:, 1, it, :], stat[:, 1, it, :]))
                rsqrt(st, n, 1)
                for it in range(TPS):
                    st(v.tensor_scalar(row[:, par, it, 0:D], h_all[:, bass.ds(TPS * n + it, 1), :].rearrange("p o d -> p (o d)"),
                                       mv[:, 1, it, 0:1], nt[:, 1, 1, it:it + 1], ALU.subtract, ALU.mult))
                st(v.tensor_copy(row[:, par, :, ROW - 1:ROW].bitcast(i32), ids_sb[:, bass.ds(TPS * n, TPS)].rearrange("p (t o) -> p t o", o=1)))
                st.end()

            def choose(n, par):
                st = Count(dve, tk, N_TK, n)
                lg = ps[:, M2, 0:TPS * E].rearrange("p (t e) -> p t e", t=TPS)
                hold(dve, g_mm, n + 1)
                for it in range(TPS):
                    st(v.max(top[:, it, :], lg[:, it, :]))
                hold(dve, tk, st.base + st.k)
                for it in range(TPS):
                    st(v.match_replace(left[:, it, :], top[:, it, :], lg[:, it, :], -BIG))
                st.wait()
                st(v.tensor_tensor(mask[:, :, :], left[:, :, :], lg, ALU.not_equal))
                st(v.tensor_scalar(ntop[:, :], top[:, :, 0], -1.0, None, ALU.mult))
                wait(dve, g_ex, TPS * (n + 1))
                st.wait()
                for it in range(TPS):
                    st(v.scalar_tensor_tensor(out=ex[:, it, :], in0=ex[:, it, :], scalar=1.0, in1=mask[:, it, :], op0=ALU.mult, op1=ALU.mult,
                                              accum_out=wsum[:, 0, it:it + 1]))
                st.wait()
                st(v.reciprocal(wsum[:, 1, :], wsum[:, 0, :]))
                st.wait()
                for it in range(TPS):
                    st(v.tensor_scalar(row[:, par, it, D:D + E], ex[:, it, :], wsum[:, 1, it:it + 1], None, ALU.mult))
                st.end()

            def place(n, par):
                st = Count(dve, ps_s, N_PS, n)
                rk = ps[:, M2, 128:128 + TPS * E].rearrange("p (t e) -> p t e", t=TPS)
                wait(dve, rk_mm, n + 1)
                st(v.tensor_tensor(posm[:, :, :], rk, base1.rearrange("p (o e) -> p o e", o=1).to_broadcast([P, TPS, E]), ALU.add))
                st(v.tensor_tensor(cum[:, :], cum[:, :], mask[:, 0, :], ALU.add))
                st.wait()
                st(v.tensor_tensor(posm[:, :, :], posm[:, :, :], mask[:, :, :], ALU.mult))
                st(v.tensor_tensor(cum[:, :], cum[:, :], mask[:, 1, :], ALU.add))
                hold(dve, ps_s, st.base + st.k)
                for it in range(TPS):
                    st(v.max(pos8[:, it, :], posm[:, it, :]))
                st.wait()
                st(v.tensor_scalar(pos[:, par, :, :], pos8[:, :, :], -1.0, None, ALU.add))
                st.end()

            hs = [0]

            def link(ins):
                hs[0] += 1
                ins.then_inc(hashed, 1)
                dve.wait_ge(hashed, hs[0])

            link(v.memset(xf[:, :], 0.0))
            dve.wait_ge(L, 16)
            link(v.tensor_copy(xf[:, 2:2 + S], xi[:, :]))
            W = S + 1
            link(v.scalar_tensor_tensor(out=hash_f[:, 0, :], in0=xf[:, 0:W], scalar=64.0, in1=xf[:, 1:1 + W], op0=ALU.mult, op1=ALU.add))
            link(v.scalar_tensor_tensor(out=hash_f[:, 1, :], in0=hash_f[:, 0, :], scalar=64.0, in1=xf[:, 2:2 + W], op0=ALU.mult, op1=ALU.add))

            def modulo(a):
                link(v.tensor_scalar(quo[:, :], a, 1.0 / VOCAB, None, ALU.mult))
                link(v.tensor_copy(quo_f[:, :], quo[:, :]))
                link(v.scalar_tensor_tensor(out=a, in0=quo_f[:, :], scalar=-float(VOCAB), in1=a, op0=ALU.mult, op1=ALU.add))
                link(v.tensor_scalar(fix[:, :], a, 0.0, float(VOCAB), ALU.is_lt, ALU.mult))
                link(v.tensor_tensor(a, a, fix[:, :], ALU.add))
                link(v.tensor_scalar(fix[:, :], a, float(VOCAB), -float(VOCAB), ALU.is_ge, ALU.mult))
                link(v.tensor_tensor(a, a, fix[:, :], ALU.add))

            modulo(hash_f[:, 1, :])
            link(v.memset(hash_f[:, 2, S:W], 0.0))
            link(v.scalar_tensor_tensor(out=hash_f[:, 2, 0:S], in0=hash_f[:, 1, 0:S], scalar=64.0, in1=xf[:, 3:3 + S], op0=ALU.mult, op1=ALU.add))
            modulo(hash_f[:, 2, :])
            dve.wait_ge(hash_t, 1)
            v.tensor_copy(idx_all[:, 0:B, :].rearrange("p b a -> p (b a)"), ps[:, M2, 0:B * TPS * NGRAMS]).then_inc(idx_ok, 1)
            v.memset(idx_all[:, B, :], 0).then_inc(idx_ok, 1)
            dve.wait_ge(idx_ok, 2)
            indices(0)
            dve.wait_ge(LC, 16 * 12)
            v.tensor_scalar(npre[:, :], pre_sb[:, :], -float(DH) ** -0.5, None, ALU.mult).then_inc(setup, 1)
            v.tensor_copy(ones_h[:, :], ones).then_inc(setup, 1)
            v.tensor_copy(before_h[:, :], before).then_inc(setup, 1)
            v.memset(cum[:, :], 0.0).then_inc(setup, 1)
            v.memset(tab_e[:, :], 0).then_inc(setup, 1)
            dve.wait_ge(setup, N_SETUP)
            edges(0)
            indices(1)
            norm1(0)
            evac_v(0, 0)
            rotate(0, 0, q_mm, q_rp, M1, q_sb, 0)
            rotate(0, 0, k_mm, k_rp, M0, k_sb, 2)
            prepare(0, 0, 0)

            def slot(b, par, s, embeds, routes):
                u = NH * b + s
                if s < NH - 1:
                    prepare(b, par, s + 1)
                maxima(u, s)
                if routes or s >= 1:
                    normalise(u - 1, (s - 1) % NH)
                if embeds and s == 0:
                    edges(b + 1)
                    indices(b + 2)
                if embeds and s == 1:
                    norm1(b + 1)
                if routes and s == 3:
                    residual_norm2(b - 1, 1 - par)
                if embeds and s == 4:
                    evac_v(b + 1, 1 - par)
                    rotate(b + 1, 1 - par, q_mm, q_rp, M1, q_sb, 0)
                if embeds and s == 5:
                    rotate(b + 1, 1 - par, k_mm, k_rp, M0, k_sb, 2)
                if routes and s == 6:
                    choose(b - 1, 1 - par)
                if routes and s == 7:
                    place(b - 1, 1 - par)
                if embeds and s == NH - 1:
                    prepare(b + 1, 1 - par, 0)

            front(nc.vector, slot)
            U = NH * B
            normalise(U - 1, 7)
            residual_norm2(B - 1, 1)
            choose(B - 1, 1)
            place(B - 1, 1)

            tk_ = [0]

            def step(ins):
                tk_[0] += 1
                ins.then_inc(tb, 1)
                dve.wait_ge(tb, tk_[0])

            dve.wait_ge(c_mm, 1)
            step(v.tensor_copy(cnt[:, :], ps[0:E, M0, 0:1]))
            step(v.tensor_tensor(offf[0:1, 0:E], ps[0:1, M1, 0:E], base1[0:1, :], ALU.add))
            step(v.tensor_scalar(cmp16[:, :], tile_lo, cnt[:, 0:1], None, ALU.is_lt))
            step(v.tensor_reduce(ntiles[:, :], cmp16[:, :], AX.X, ALU.add))
            step(v.tensor_scalar(gap[:, :], ntiles[:, :], -float(P), float(CAP), ALU.mult, ALU.add))
            step(v.tensor_scalar(tab_pad[:, :], offf[0:1, 0:E], -1.0, None, ALU.add))
            dve.wait_ge(c_mm, 2)
            step(v.tensor_copy(ends[:, :], ps[0:E, M2, 0:1]))
            step(v.memset(cmp16[:, 0:1], 0.0))
            step(v.tensor_scalar(past[:, :], tile_no, ends[:, 0:1], None, ALU.is_ge))
            dve.wait_ge(c_mm, 3)
            step(v.scalar_tensor_tensor(out=offf[:, :], in0=tile_no[0:1, :], scalar=float(P), in1=ps[0:1, M1, 0:TILES], op0=ALU.mult, op1=ALU.add))
            step(v.tensor_scalar(tab_off[:, :], offf[:, :], float(DUMMY), None, ALU.min))
            step(v.tensor_scalar(tab_e[:, 2:2 + TILES], ps[0:1, M0, 0:TILES], float(E - 1), None, ALU.min))

            for c in range(T // SHC):
                for m, (lo, w) in enumerate(SHM):
                    wait(dve, sha, 3 * c + m + 1)
                    wait(dve, shy, c)
                    v.tensor_tensor(sh_hid[0:w, m, :], sh_g[0:w, :], ps[0:w, 2 * (m % 2) + 1, :], ALU.mult).then_inc(shh, 1)
                wait(dve, shy, c + 1)
                hc = h_all[:, c * (SHC // P):(c + 1) * (SHC // P), :].rearrange("p t d -> p (t d)")
                v.tensor_tensor(hc, ps[:, OB, :], hc, ALU.add).then_inc(she, 1)

            def tile_evac(q, k):
                wait(dve, x_tr, q + 1)
                wait(dve, h_mm, q - 1)
                v.tensor_copy(x_t[:, k % 2, :, :].rearrange("p t n -> p (t n)"), ps[:, k % 2, 0:2 * P]).then_inc(x_ev, 1)

            def gated(q, k):
                wait(dve, h_si, q + 1)
                wait(dve, h_tr, q - 1)
                v.tensor_tensor(hid[:, k % 2, :, :], sg[:, k % 2, :, :],
                                ps[:, 2 + k % 2, :].rearrange("p (t a n) -> p t a n", t=2, a=2)[:, :, 1, :], ALU.mult).then_inc(h_mu, 1)

            def weighted(q, k, e):
                wait(dve, y_mm, q + 1)
                for t in range(2):
                    v.tensor_scalar(y_sb[:, 2 * k + t, :], ps[:, 6 + k % 2, t * D:(t + 1) * D],
                                    rows[:, 2 * k + t, bass.ds(e[t] + D, 1)], None, ALU.mult).then_inc(y_ev, 1)

            def group(j, first, last):
                q = PAIRS * j
                e = table(tab_e[0:1, bass.ds(RING * j, RING + (2 if last else 0))], mybir.EngineType.DVE, E - 1)
                if first:
                    tile_evac(0, 0)
                    tile_evac(1, 1)
                    gated(0, 0)
                for k in range(PAIRS):
                    if not (last and k >= PAIRS - 2):
                        tile_evac(q + k + 2, (k + 2) % PAIRS)
                    if not (last and k == PAIRS - 1):
                        gated(q + k + 1, (k + 1) % PAIRS)
                    if not (first and k == 0):
                        weighted(q + k - 1, (k - 1) % PAIRS, e[2 * k:2 * k + 2])
                if last:
                    weighted(q + PAIRS - 1, PAIRS - 1, e[RING:RING + 2])

            group(0, True, False)
            with nc.vector.Fori(1, GROUPS - 1) as j:
                group(j, False, False)
            group(GROUPS - 1, False, True)

            dve.wait_ge(acc_ld, 16 * ACCS)
            for g in range(4):
                t = slice(4 * g, 4 * g + 4)
                for r in range(ACCS):
                    if r:
                        dve.wait_ge(fin, ACCS * g + r)
                    v.tensor_tensor(h_all[:, t, :], h_all[:, t, :], acc_in[:, r, t, :], ALU.add).then_inc(fin, 1)


_OUT = (B, S, D)


def kernel(**inputs):
    import concourse.bacc as bacc
    from concourse.bass_utils import run_bass_kernel_spmd as run

    g = {k: np.asarray(a) for k, a in inputs.items()}
    f = np.float32
    wq, wk, wv = (g["L0_attn_w_qkv"][i * D:(i + 1) * D] for i in range(3))
    bq, bk, bv = (g["L0_attn_b_qkv"][i * D:(i + 1) * D] for i in range(3))
    swap = np.arange(D).reshape(NH, 4, DH // 4)[:, [1, 0, 3, 2]].reshape(D)
    inv = (1.0 / 10000.0 ** (np.arange(0, DH, 4, dtype=f) / DH)).astype(f)
    pos = np.arange(S, dtype=f)
    local = (pos % 64)[None, :] * inv[:, None]
    chunk = np.floor(pos / 64)[None, :] * inv[:, None]
    ang = np.stack([local, local, chunk, chunk])
    sign = np.array([-1, 1, -1, 1], f)[:, None, None]
    rope = np.stack([np.tile(np.cos(ang).reshape(DH, S), (NH, 1)),
                     np.tile((sign * np.sin(ang)).reshape(DH, S), (NH, 1))]).astype(f)
    p = np.arange(P)
    padding = np.zeros((P, ROW), f)
    padding[:, ROW - 1] = (T + p).astype(np.int32).view(f)
    consts = np.concatenate([np.eye(P, dtype=f), np.ones((P, P), f), (p[:, None] < p[None, :]).astype(f),
                             np.tile((np.arange(E) * CAP + 1).astype(f), (P, 1)), padding], axis=1)
    e = np.arange(E)
    iotas = np.concatenate([np.tile(np.arange(TILES, dtype=f), (E, 1)), np.tile(P * np.arange(16, dtype=f), (E, 1)),
                            (e[:, None] <= e[None, :]).astype(f)], axis=1)
    args = {
        "x": g["x"], "emb2": g["L0_tok_emb_2"], "emb3": g["L0_tok_emb_3"], "emb4": g["L0_tok_emb_4"],
        "w1": g["L0_ffn_w1"], "w3": g["L0_ffn_w3"], "w2": g["L0_ffn_w2"],
        "sw1": g["L0_ffn_sw1"], "sw3": g["L0_ffn_sw3"], "sw2": g["L0_ffn_sw2"],
        "proj_t": g["L0_tok_proj_w"].T,
        "qkv_t": np.concatenate([wq.T, wq[swap].T, wk.T, wk[swap].T, wv.T], axis=1),
        "out_t": g["L0_attn_w_out"].T, "gate_t": g["L0_ffn_gate_w"].T,
        "bias_rows": np.stack([g["L0_tok_proj_b"], bv, g["L0_attn_b_out"]]),
        "bias_cols": np.stack([bq, bq[swap], bk, bk[swap]], axis=1),
        "pre_cols": np.repeat(g["L0_attn_w_pre"].T, DH, axis=0),
        "post_row": np.repeat(g["L0_attn_w_post"].T, DH, axis=1).reshape(1, NH, D),
        "rope": rope, "consts": consts, "iotas": iotas,
        "ids": (np.arange(NT)[None, :] * P + p[:, None]).astype(np.int32),
    }
    nc = bacc.Bacc("TRN2", target_bir_lowering=False, num_devices=1)
    arrays, aps = {}, []
    for name, a in args.items():
        a = np.ascontiguousarray(a)
        arrays[f"in_{name}"] = a
        aps.append(nc.dram_tensor(f"in_{name}", a.shape, mybir.dt.from_np(a.dtype), kind="ExternalInput").ap())
    aps.append(nc.dram_tensor("out_0", _OUT, f32, kind="ExternalOutput").ap())
    tower(nc, *aps)
    r = run(nc, [arrays], core_ids=[0])
    return r.results[0]["out_0"]
```
